# Optimizing a Trainium2 kernel written in Bass

```python
import numpy as np
import jax
import jax.numpy as jnp

def _softmax(x, axis=-1):
    return jax.nn.softmax(x, axis=axis)

def _gelu(x):
    return jax.nn.gelu(x, approximate=True)

def _silu(x):
    return jax.nn.silu(x)

def _sigmoid(x):
    return jax.nn.sigmoid(x)

def _layernorm(x, axis=-1, eps=1e-05):
    m = jnp.mean(x, axis=axis, keepdims=True)
    v = jnp.var(x, axis=axis, keepdims=True)
    return (x - m) / jnp.sqrt(v + eps)

def _scatter_add(tgt, idx, src, axis=0):
    return tgt.at[idx].add(src)

def _segment_sum(src, seg, n):
    return jax.ops.segment_sum(src, seg, n)
kernel_name = 'mk_adj_resnorm_d2_adj_r2_d6f531'

def setup_inputs(seed: int=0):
    np.random.seed(seed)
    _w = jnp.asarray

    def _rec_inputs():
        import jax
        import jax.numpy as jnp
        _gk = jax.random.key(seed)
        x = -0.000929 + 1 * jax.random.normal(jax.random.fold_in(_gk, 1), (8, 1024, 64), jnp.float32)
        _w = (1.0 + jnp.arange(1024, dtype=jnp.float32)) ** (-0.5)
        _w = _w / _w.mean()
        _pij = jnp.clip(0.0078125 * _w[:, None] * _w[None, :], 0.0, 1.0)
        _a = jax.random.uniform(jax.random.fold_in(_gk, 2), (8, 1024, 1024)) < _pij
        _a = jnp.logical_or(_a, jnp.swapaxes(_a, -1, -2))
        _a = jnp.logical_or(_a, jnp.eye(1024, dtype=bool))
        _af = _a.astype(jnp.float32)
        _af = _af * jax.random.uniform(jax.random.fold_in(_gk, 3), (8, 1024, 1024), jnp.float32, 0.05, 1)
        adj = _af
        _nm = jnp.ones((8, 1024), dtype=bool)
        nodemask = _nm
        return (x, adj, nodemask)
    x, adj, nodemask = _rec_inputs()

    def _L0_gnn_setup():
        import jax, jax.numpy as jnp
        import numpy as np
        B, N, IN_C, OUT_C, K_ORDERS = (16, 512, 64, 64, 4)

        def _get_laplacian(graph):
            deg = jnp.sum(graph, axis=-1)
            d = deg ** (-0.5)
            d = jnp.where(jnp.isnan(d), 0.0, d)
            eye = jnp.eye(graph.shape[1], dtype=graph.dtype)
            L = eye[None] - d[:, :, None] * graph * d[:, None, :]
            L = jnp.where(jnp.isnan(L), 0.0, L)
            L = jnp.where(jnp.isinf(L), 0.0, L)
            return L

        def _cheb_polynomials(L, k_orders):
            b, n = (L.shape[0], L.shape[1])
            T0 = jnp.broadcast_to(jnp.eye(n, dtype=L.dtype)[None], (b, n, n))
            Ts = [T0]
            if k_orders > 1:
                Ts.append(L)
                for _ in range(2, k_orders):
                    Ts.append(2.0 * jnp.matmul(L, Ts[-1]) - Ts[-2])
            return jnp.stack(Ts, axis=0)
        key = jax.random.key(seed)
        k1, k2, k3, k4 = jax.random.split(key, 4)
        inputs = jax.random.normal(k1, (B, N, IN_C), dtype=jnp.float32)
        graph = jax.random.uniform(k2, (B, N, N), dtype=jnp.float32)
        std = float(np.sqrt(2.0 / (IN_C + OUT_C)))
        weight = jax.random.normal(k3, (K_ORDERS, 1, IN_C, OUT_C), dtype=jnp.float32) * std
        bias = jax.random.normal(k4, (1, 1, OUT_C), dtype=jnp.float32) * 0.01
        return {'inputs': inputs, 'graph': graph, 'weight': weight, 'bias': bias}
    _L0_gnn_all = _L0_gnn_setup()
    _L0_gnn_in = {k: v for k, v in _L0_gnn_all.items() if k in ('weight', 'bias')}
    del _L0_gnn_all

    def _L1_gnn_setup():
        import jax, jax.numpy as jnp
        import numpy as np
        TAUS = [0.25, 0.5, 0.75]
        QWEIGHTS = [0.25, 0.5, 0.25]
        T_THRESH = 10
        K_DIL = 2
        EPS_GIN = 0.0

        def _dilate_adj(adj, mask):
            B, N, _ = adj.shape
            eye = jnp.eye(N, dtype=bool)
            adj_ = jnp.where(eye[None], 1.0, adj)
            nb = (adj_ > 0) & (~eye)[None]
            m = nb.sum(-1)
            rank = jnp.cumsum(nb, axis=-1) - 1
            skip = jnp.where(m > T_THRESH, (m + K_DIL - 1) // K_DIL, 1)
            do_dil = (skip > 1) & mask
            removed = nb & do_dil[..., None] & ((rank + 1) % skip[..., None] == 0)
            rem = removed | jnp.swapaxes(removed, 1, 2)
            return jnp.where(rem, 0.0, adj_)

        def _weighted_nanquantile_agg(x, valid):
            B, N, C = x.shape
            big = jnp.finfo(x.dtype).max / 4
            vals = jnp.where(valid[..., None], x[:, None, :, :], big)
            sv = jnp.sort(vals, axis=2)
            m = valid.sum(-1)
            mf = m.astype(x.dtype)

            def gather(idx):
                idxb = jnp.broadcast_to(idx[:, :, None, None], (B, N, 1, C))
                return jnp.take_along_axis(sv, idxb, axis=2)[:, :, 0, :]
            agg = jnp.zeros_like(x)
            for tau, wt in zip(TAUS, QWEIGHTS):
                pos = jnp.clip(tau * (mf - 1.0), 0.0)
                lo = jnp.floor(pos).astype(jnp.int32)
                hi = jnp.ceil(pos).astype(jnp.int32)
                frac = (pos - lo.astype(x.dtype))[..., None]
                q = gather(lo) * (1.0 - frac) + gather(hi) * frac
                agg = agg + wt * q
            return jnp.where((m > 0)[..., None], agg, 0.0)
        key = jax.random.key(seed)
        k0, k1, k2, k3 = jax.random.split(key, 4)
        B, N, C, H, CO = (4, 256, 64, 128, 64)
        x = jax.random.normal(k0, (B, N, C), dtype=jnp.float32)
        u = jax.random.uniform(k1, (B, N, N))
        a = (u < 0.03).astype(jnp.float32)
        adj = jnp.maximum(a, jnp.swapaxes(a, 1, 2))
        mask = jnp.broadcast_to(jnp.arange(N) < N - 32, (B, N))
        W1 = jax.random.normal(k2, (C, H), dtype=jnp.float32) * (1.0 / np.sqrt(C))
        b1 = jnp.zeros((H,), dtype=jnp.float32)
        W2 = jax.random.normal(k3, (H, CO), dtype=jnp.float32) * (1.0 / np.sqrt(H))
        b2 = jnp.zeros((CO,), dtype=jnp.float32)
        return {'x': x, 'adj': adj, 'mask': mask, 'W1': W1, 'b1': b1, 'W2': W2, 'b2': b2}
    _L1_gnn_all = _L1_gnn_setup()
    _L1_gnn_in = {k: v for k, v in _L1_gnn_all.items() if k in ('W1', 'b1', 'W2', 'b2')}
    del _L1_gnn_all
    return {'x': x, 'adj': adj, 'nodemask': nodemask, 'L0_gnn_weight': _L0_gnn_in['weight'], 'L0_gnn_bias': _L0_gnn_in['bias'], 'L1_gnn_W1': _L1_gnn_in['W1'], 'L1_gnn_b1': _L1_gnn_in['b1'], 'L1_gnn_W2': _L1_gnn_in['W2'], 'L1_gnn_b2': _L1_gnn_in['b2']}

def reference(x, adj, nodemask, L0_gnn_weight, L0_gnn_bias, L1_gnn_W1, L1_gnn_b1, L1_gnn_W2, L1_gnn_b2):
    import jax
    import jax.numpy as jnp

    def _L0_gnn_ref(inputs, graph, weight, bias):
        import jax, jax.numpy as jnp
        import numpy as np
        B, N, IN_C, OUT_C, K_ORDERS = (16, 512, 64, 64, 4)

        def _get_laplacian(graph):
            deg = jnp.sum(graph, axis=-1)
            d = deg ** (-0.5)
            d = jnp.where(jnp.isnan(d), 0.0, d)
            eye = jnp.eye(graph.shape[1], dtype=graph.dtype)
            L = eye[None] - d[:, :, None] * graph * d[:, None, :]
            L = jnp.where(jnp.isnan(L), 0.0, L)
            L = jnp.where(jnp.isinf(L), 0.0, L)
            return L

        def _cheb_polynomials(L, k_orders):
            b, n = (L.shape[0], L.shape[1])
            T0 = jnp.broadcast_to(jnp.eye(n, dtype=L.dtype)[None], (b, n, n))
            Ts = [T0]
            if k_orders > 1:
                Ts.append(L)
                for _ in range(2, k_orders):
                    Ts.append(2.0 * jnp.matmul(L, Ts[-1]) - Ts[-2])
            return jnp.stack(Ts, axis=0)
        L = _get_laplacian(graph)
        mul_l = _cheb_polynomials(L, K_ORDERS)
        res = jnp.einsum('kbnm,bmc->kbnc', mul_l, inputs)
        out = jnp.einsum('kbnc,kco->bno', res, weight[:, 0])
        return out + bias

    def _L1_gnn_ref(x, adj, mask, W1, b1, W2, b2):
        import jax, jax.numpy as jnp
        import numpy as np
        TAUS = [0.25, 0.5, 0.75]
        QWEIGHTS = [0.25, 0.5, 0.25]
        T_THRESH = 10
        K_DIL = 2
        EPS_GIN = 0.0

        def _dilate_adj(adj, mask):
            B, N, _ = adj.shape
            eye = jnp.eye(N, dtype=bool)
            adj_ = jnp.where(eye[None], 1.0, adj)
            nb = (adj_ > 0) & (~eye)[None]
            m = nb.sum(-1)
            rank = jnp.cumsum(nb, axis=-1) - 1
            skip = jnp.where(m > T_THRESH, (m + K_DIL - 1) // K_DIL, 1)
            do_dil = (skip > 1) & mask
            removed = nb & do_dil[..., None] & ((rank + 1) % skip[..., None] == 0)
            rem = removed | jnp.swapaxes(removed, 1, 2)
            return jnp.where(rem, 0.0, adj_)

        def _weighted_nanquantile_agg(x, valid):
            B, N, C = x.shape
            big = jnp.finfo(x.dtype).max / 4
            vals = jnp.where(valid[..., None], x[:, None, :, :], big)
            sv = jnp.sort(vals, axis=2)
            m = valid.sum(-1)
            mf = m.astype(x.dtype)

            def gather(idx):
                idxb = jnp.broadcast_to(idx[:, :, None, None], (B, N, 1, C))
                return jnp.take_along_axis(sv, idxb, axis=2)[:, :, 0, :]
            agg = jnp.zeros_like(x)
            for tau, wt in zip(TAUS, QWEIGHTS):
                pos = jnp.clip(tau * (mf - 1.0), 0.0)
                lo = jnp.floor(pos).astype(jnp.int32)
                hi = jnp.ceil(pos).astype(jnp.int32)
                frac = (pos - lo.astype(x.dtype))[..., None]
                q = gather(lo) * (1.0 - frac) + gather(hi) * frac
                agg = agg + wt * q
            return jnp.where((m > 0)[..., None], agg, 0.0)
        dtp = x.dtype
        adj_d = _dilate_adj(adj, mask)
        agg = _weighted_nanquantile_agg(x, adj_d > 0)
        out = (1.0 + EPS_GIN) * x + agg
        h = jax.nn.relu(jnp.einsum('bnc,ch->bnh', out, W1) + b1)
        y = jnp.einsum('bnh,ho->bno', h, W2) + b2
        return y * mask[..., None].astype(dtp)
    x = _layernorm(x + _L0_gnn_ref(x, adj, L0_gnn_weight, L0_gnn_bias), axis=-1)
    x = _layernorm(x + _L1_gnn_ref(x, adj, nodemask, L1_gnn_W1, L1_gnn_b1, L1_gnn_W2, L1_gnn_b2), axis=-1)
    return x

_drawn_inputs = setup_inputs


def setup_inputs(seed=0):
    import zlib

    import numpy as np

    out = dict(_drawn_inputs(seed))
    spreads = {'L1_gnn_b1': (0.0, 0.1), 'L1_gnn_b2': (0.0, 0.1)}
    factors = {'L0_gnn_bias': 8.0}
    for name, (base, spread) in spreads.items():
        noise = np.random.default_rng([zlib.crc32(name.encode()), seed]).standard_normal(out[name].shape)
        drawn = base * np.exp(spread * noise) if base else spread * noise
        out[name] = jnp.asarray(drawn.astype(out[name].dtype))
    for name, factor in factors.items():
        out[name] = (out[name] * factor).astype(out[name].dtype)
    return out
```

```python
from contextlib import ExitStack

import concourse.bass as bass
from concourse import mybir

F32 = mybir.dt.float32
F16 = mybir.dt.float16
BF16 = mybir.dt.bfloat16
I32 = mybir.dt.int32
U32 = mybir.dt.uint32
U8 = mybir.dt.uint8
ALU = mybir.AluOpType
ACT = mybir.ActivationFunctionType
AX_X = mybir.AxisListType.X

P = 128
EPS = 1e-5
T_THRESH = 10
TAUS = (0.25, 0.5, 0.75)
QWEIGHTS = (0.25, 0.5, 0.25)
PAD_VALUE = 1e30
WIDE = (16, 32, 64)
NARROW = (128, 256, 512, 1024)
LEVELS = WIDE + NARROW
GROUPS = 8
NARROW_NODES = P // GROUPS
BLOCK = 64
META = 16


def sort_stages(n):
    p = 1
    while p < n:
        k = p
        while k >= 1:
            yield p, k
            k //= 2
        p *= 2


def build(nc, x, xT, adj, adjT, mask, w_cat, bias0, W1, b1, W2, b2, out):
    B, N, C = x.shape
    H = W1.shape[1]
    T = N // P
    NODES = B * N
    COLS = NODES // P
    LIST = NODES + P
    K0 = w_cat.shape[1] // C

    key_rows = nc.dram_tensor("key_rows", (NODES + 1, N), F16, kind="Internal").ap()
    x1_rows = nc.dram_tensor("x1_rows", (NODES + 1, C), F32, kind="Internal").ap()
    agg_rows = nc.dram_tensor("agg_rows", (NODES, C), F32, kind="Internal").ap()
    meta_rows = nc.dram_tensor("meta_rows", (NODES + P, META), F32, kind="Internal").ap()
    lists = nc.dram_tensor("lists", (len(LEVELS) * LIST, 1), I32, kind="Internal").ap()

    with ExitStack() as ctx:
        def sb(name, shape, dt):
            return ctx.enter_context(nc.sbuf_tensor(name, shape, dt))

        def ps(name, shape, dt=F32):
            return ctx.enter_context(nc.psum_tensor(name, shape, dt))

        def sem(name):
            return ctx.enter_context(nc.semaphore(name))

        diff = sb("diff", [P, P], I32)
        ident = sb("ident", [P, P], F32)
        ident_b = sb("ident_b", [P, P], BF16)
        off_diag = sb("off_diag", [P, P], F16)
        before = sb("before", [P, P], F32)
        ones = sb("ones", [P, P], F32)
        ramp_i = sb("ramp_i", [P, N], I32)
        down = sb("down", [P, N], F16)
        up = sb("up", [P, N], F32)
        diag_key = sb("diag_key", [P, N], F16)
        ones_row = sb("ones_row", [P, N], F16)
        part_i = sb("part_i", [P, 1], I32)
        group_f = sb("group_f", [P, 1], F32)
        eps_t = sb("eps_t", [P, T], F32)
        power = sb("power", [P, T], F32)
        wcat_sb = sb("wcat_sb", [C, K0 * C], F32)
        bias0_sb = sb("bias0_sb", [P, C], F32)
        W1_sb = sb("W1_sb", [C, H], F32)
        b1_sb = sb("b1_sb", [H, 1], F32)
        W2_sb = sb("W2_sb", [H, C], F32)
        b2_sb = sb("b2_sb", [P, C], F32)
        mask_u = sb("mask_u", [P, COLS], U8)
        mask_f = sb("mask_f", [P, COLS], F32)
        m_all = sb("m_all", [P, COLS], F32)
        tiles_of = sb("tiles_of", [P, len(LEVELS)], I32)

        slots = [sb(f"slots{i}", [P, T * N], F32) for i in range(2)]

        def rows(ap, first, n):
            return ap[first:first + n, :]

        step = sem("step")

        with ExitStack() as sctx:
            loaded = sctx.enter_context(nc.semaphore("weights_loaded"))
            iotas = sctx.enter_context(nc.semaphore("iotas_done"))
            consts = sctx.enter_context(nc.semaphore("consts_done"))
            pad_stored = sctx.enter_context(nc.semaphore("pad_stored"))
            pad_f = sctx.enter_context(nc.sbuf_tensor("pad_f", [1, C], F32))
            pad_k = sctx.enter_context(nc.sbuf_tensor("pad_k", [1, N], F16))
            block = sctx.enter_context(nc.Block())

            @block.sync
            def _(sp):
                sp.dma_start(wcat_sb[:], w_cat).then_inc(loaded, 16)
                sp.dma_start(bias0_sb[:], bias0.partition_broadcast(P)).then_inc(loaded, 16)
                sp.dma_start(W1_sb[:], W1).then_inc(loaded, 16)
                sp.dma_start(b1_sb[:], b1).then_inc(loaded, 16)
                sp.dma_start(W2_sb[:], W2).then_inc(loaded, 16)
                sp.dma_start(b2_sb[:], b2.partition_broadcast(P)).then_inc(loaded, 16)
                sp.dma_start(mask_u[:], mask).then_inc(loaded, 16)
                sp.wait_ge(consts, 1)
                sp.dma_start(rows(x1_rows, NODES, 1), pad_f[:]).then_inc(pad_stored, 16)
                sp.dma_start(rows(key_rows, NODES, 1), pad_k[:]).then_inc(pad_stored, 16)
                sp.wait_ge(pad_stored, 32)
                sp.wait_ge(loaded, 16 * 7)

            @block.gpsimd
            def _(pool):
                nc.gpsimd.iota(diff[:], pattern=[[1, P]], base=0, channel_multiplier=-1).then_inc(iotas, 1)
                nc.gpsimd.iota(ramp_i[:], pattern=[[1, N]], base=0, channel_multiplier=0).then_inc(iotas, 1)
                nc.gpsimd.iota(part_i[:], pattern=[[0, 1]], base=0, channel_multiplier=1).then_inc(iotas, 1)

            @block.vector
            def _(dve):
                count = [0]

                def done(*instructions):
                    for i in instructions:
                        i.then_inc(step, 1)
                    count[0] += len(instructions)
                    dve.wait_ge(step, count[0])

                dve.wait_ge(iotas, 3)
                dve.wait_ge(loaded, 16 * 7)
                v = nc.vector
                done(
                    v.tensor_scalar(ident[:], diff[:], 0, None, ALU.is_equal),
                    v.tensor_scalar(ident_b[:], diff[:], 0, None, ALU.is_equal),
                    v.tensor_scalar(off_diag[:], diff[:], 0, None, ALU.not_equal),
                    v.tensor_scalar(before[:], diff[:], 0, None, ALU.is_gt),
                    v.memset(ones[:], 1.0),
                    v.memset(ones_row[:], 1.0),
                    v.memset(eps_t[:], EPS),
                    v.memset(power[:], -0.5),
                    v.memset(pad_f[:], PAD_VALUE),
                    v.memset(pad_k[:], 0.0),
                    v.tensor_scalar(down[:], ramp_i[:], -1.0, float(N), ALU.mult, ALU.add),
                    v.tensor_copy(up[:], ramp_i[:]),
                    v.tensor_scalar(part_i[:], part_i[:], 4, None, ALU.logical_shift_right),
                    v.tensor_copy(mask_f[:], mask_u[:]),
                )
                done(v.tensor_copy(group_f[:], part_i[:]),
                     *[v.tensor_tensor(diag_key[:, bass.ts(t, P)], down[:, bass.ts(t, P)], ident_b[:], ALU.mult)
                       for t in range(T)])
                dve.sem_inc(consts, 1)
                dve.sem_clear(step)

        with ExitStack() as actx:
            def asb(name, shape, dt):
                return actx.enter_context(nc.sbuf_tensor(name, shape, dt))

            def asem(name):
                return actx.enter_context(nc.semaphore(name))

            adj_sb = slots[0][:].rearrange("p (t n) -> p t n", t=T)
            adjT_sb = slots[1][:].rearrange("p (t n) -> p t n", t=T)
            x_sb = asb("x_sb", [P, T, C], F32)
            xT_sb = asb("xT_sb", [C, N], F32)
            nbkey = asb("nbkey", [P, T, N], F16)
            ranked = asb("ranked", [P, T, N], F16)
            removed = asb("removed", [P, T, N], BF16)
            nb = asb("nb", [P, N], F16)
            rank = asb("rank", [P, N], F16)
            first_hit = asb("first_hit", [P, N], BF16)
            key_out = asb("key_out", [P, 2, N], F16)
            act_junk = asb("act_junk", [P, N], BF16)
            deg = asb("deg", [P, T], F32)
            safe_deg = asb("safe_deg", [P, T], F32)
            dpow = asb("dpow", [P, T], F32)
            dsc = asb("dsc", [P, T], F32)
            keep = asb("keep", [P, T], F32)
            m_batch = asb("m_batch", [P, T], F32)
            nb_count = asb("nb_count", [P, T], F32)
            count_i = asb("count_i", [P, T], I32)
            half_i = asb("half_i", [P, T], I32)
            odd_i = asb("odd_i", [P, T], I32)
            hit1 = asb("hit1", [P, T], F32)
            hit2 = asb("hit2", [P, T], F32)
            dil = asb("dil", [P, T], F32)
            mask_b = asb("mask_b", [P, T], F32)
            even = asb("even", [P, T], F32)
            proj = asb("proj", [P, T, K0 * C], F32)
            z = asb("z", [P, T, C], F32)
            bb = [asb(f"bb{i}", [P, T, C], F32) for i in range(3)]
            tmp = asb("tmp", [P, T, C], F32)
            tmp2 = asb("tmp2", [P, T, C], F32)
            mean = asb("mean", [P, T], F32)
            var = asb("var", [P, T], F32)
            rstd = asb("rstd", [P, T], F32)
            x1_sb = asb("x1_sb", [P, T, C], F32)

            proj_ps = actx.enter_context(nc.psum_tensor("proj_ps", [P, T // 2, K0 * C], F32))
            y_ps = actx.enter_context(nc.psum_tensor("y_ps", [P, T, C], F32))
            rem_ps = [actx.enter_context(nc.psum_tensor(f"rem_ps{i}", [P, N], F32)) for i in range(2)]

            names = ("adj_loaded adjT_loaded x_loaded adj_for_dve adj_for_act adj_free adjT_free x_free "
                     "deg_ready pow_ready safe_ready var_ready rstd_ready half_projected half_copied proj_ready z_ready y_ready "
                     "removed_ready rem_ready0 rem_ready1 rem_free0 rem_free1 key_ready0 key_ready1 key_for_act0 "
                     "key_for_act1 key_counted0 key_counted1 key_stored0 key_stored1 x1_ready x1_stored m_ready").split()
            s = {n: asem(n) for n in names}
            astep = asem("astep")
            astep_pe = asem("astep_pe")
            block = actx.enter_context(nc.Block())

            def take(eng, name, n=1):
                eng.wait_ge(s[name], n)
                eng.sem_clear(s[name])

            @block.sync
            def _(sp):
                with sp.Fori(0, B) as b:
                    take(sp, "adj_free", 2)
                    sp.dma_start(adj_sb, adj[bass.ds(b, 1)].rearrange("o (t p) n -> p (o t) n", p=P)).then_inc(
                        s["adj_loaded"], 16)
                    take(sp, "x_free", 2)
                    xr = x[bass.ds(b, 1)].rearrange("o (t p) c -> p (o t) c", p=P)
                    sp.dma_start(x_sb[:], xr).then_inc(s["x_loaded"], 16)
                    sp.dma_start(xT_sb[:], xT[bass.ds(b, 1)].rearrange("o c n -> (o c) n")).then_inc(s["x_loaded"], 16)
                    take(sp, "adjT_free")
                    sp.dma_start(adjT_sb, adjT[bass.ds(b, 1)].rearrange("o (t p) n -> p (o t) n", p=P)).then_inc(
                        s["adjT_loaded"], 16)
                    take(sp, "adj_loaded", 16)
                    sp.sem_inc(s["adj_for_dve"], 1)
                    sp.sem_inc(s["adj_for_act"], 1)
                    for t in range(T):
                        q = t % 2
                        take(sp, f"key_ready{q}")
                        sp.dma_start(key_rows[bass.ds(b * N + t * P, P)], key_out[:, q, :]).then_inc(
                            s[f"key_stored{q}"], 16)
                        if t == 3:
                            take(sp, "x1_ready")
                            dst = x1_rows[bass.ds(b * N, N)].rearrange("(t p) c -> p t c", p=P)
                            sp.dma_start(dst, x1_sb[:]).then_inc(s["x1_stored"], 16)
                            

            @block.scalar
            def _(act):
                a = nc.scalar
                act.sem_inc(s["adj_free"], 1)
                with act.Fori(0, B) as b:
                    take(act, "adj_for_act")
                    for t in range(T):
                        last = a.activation(act_junk[:], adj_sb[:, t, :], ACT.Copy, accum_out=deg[:, t:t + 1])
                        last.then_inc(astep, 1)
                        act.wait_ge(astep, t + 1)
                    act.sem_inc(s["adj_free"], 1)
                    act.sem_inc(s["deg_ready"], 1)
                    act.sem_clear(astep)
                    for h in range(2):
                        take(act, "half_projected")
                        a.copy(proj[:, bass.ts(h, T // 2), :], proj_ps[:]).then_inc(astep, 1)
                        act.wait_ge(astep, h + 1)
                        act.sem_inc(s["half_copied"], 1)
                    act.sem_inc(s["proj_ready"], 1)
                    act.sem_clear(astep)
                    for t in range(T):
                        q = t % 2
                        take(act, f"key_for_act{q}")
                        a.activation(act_junk[:], key_out[:, q, :], ACT.Sign,
                                     accum_out=m_batch[:, t:t + 1]).then_inc(astep, 1)
                        act.wait_ge(astep, t + 1)
                        act.sem_inc(s[f"key_counted{q}"], 1)
                    act.sem_clear(astep)
                    a.copy(m_all[:, bass.ds(b * T, T)], m_batch[:]).then_inc(astep, 1)
                    act.wait_ge(astep, 1)
                    act.sem_clear(astep)

            @block.gpsimd
            def _(pool):
                with pool.Fori(0, B) as b:
                    take(pool, "safe_ready")
                    nc.gpsimd.tensor_tensor(dpow[:], safe_deg[:], power[:], ALU.pow).then_inc(s["pow_ready"], 1)
                    take(pool, "var_ready")
                    nc.gpsimd.tensor_tensor(rstd[:], var[:], power[:], ALU.pow).then_inc(s["rstd_ready"], 1)

            @block.tensor
            def _(pe):
                pe.sem_inc(s["adjT_free"], 1)
                pe.sem_inc(s["x_free"], 1)
                with pe.Fori(0, B) as b:
                    take(pe, "x_loaded", 32)
                    for h in range(2):
                        for u in range(T // 2):
                            mm = nc.tensor.matmul(proj_ps[:, u, :], xT_sb[:, bass.ts(h * T // 2 + u, P)], wcat_sb[:],
                                                  start=True, stop=True)
                        mm.then_inc(s["half_projected"], 1)
                        take(pe, "half_copied")
                    pe.sem_inc(s["x_free"], 1)
                    take(pe, "adjT_loaded", 16)
                    for r in range(K0 - 1):
                        take(pe, "z_ready")
                        for t in range(T):
                            for j in range(T):
                                mm = nc.tensor.matmul(y_ps[:, t, :], adjT_sb[:, j, bass.ts(t, P)], z[:, j, :],
                                                      start=(j == 0), stop=(j == T - 1))
                        mm.then_inc(s["y_ready"], 1)
                    mm = nc.tensor.matmul(proj_ps[:, 0, 0:C], ident[:], ones[:, 0:C], start=True, stop=True)
                    mm.then_inc(astep_pe, 1)
                    pe.wait_ge(astep_pe, 1)
                    pe.sem_clear(astep_pe)
                    pe.sem_inc(s["adjT_free"], 1)
                    take(pe, "removed_ready")
                    for t in range(T):
                        q = t % 2
                        take(pe, f"rem_free{q}")
                        for g in range(2):
                            half = rem_ps[q][:, bass.ts(g, 512)]
                            nc.tensor.matmul(half, ident_b[:], removed[:, t, bass.ts(g, 512)], start=True, stop=False)
                            for j in range(4):
                                mm = nc.tensor.matmul(half[:, bass.ts(j, P)], removed[:, g * 4 + j, bass.ts(t, P)],
                                                      ident_b[:], start=False, stop=(j == 3))
                        mm.then_inc(s[f"rem_ready{q}"], 1)

            @block.vector
            def _(dve):
                v = nc.vector
                count = [0]

                def done(*instructions):
                    for i in instructions:
                        i.then_inc(step, 1)
                    count[0] += len(instructions)
                    dve.wait_ge(step, count[0])

                def wide(ap):
                    return ap.unsqueeze(2).to_broadcast([P, T, C])

                def apply_laplacian(src, add_to, factor, minus, dst):
                    take(dve, "y_ready")
                    done(v.tensor_tensor(tmp[:], y_ps[:], wide(dsc[:]), ALU.mult),
                         v.tensor_tensor(tmp2[:], src, wide(keep[:]), ALU.mult))
                    done(v.tensor_tensor(tmp[:], tmp2[:], tmp[:], ALU.subtract))
                    done(v.scalar_tensor_tensor(out=dst, in0=tmp[:], scalar=factor, in1=add_to, op0=ALU.mult,
                                                op1=ALU.add))
                    if minus is not None:
                        done(v.tensor_tensor(dst, dst, minus, ALU.subtract))

                def start_product(src):
                    done(v.tensor_tensor(z[:], src, wide(dsc[:]), ALU.mult))
                    dve.sem_inc(s["z_ready"], 1)

                def order(k):
                    return proj[:, :, k * C:(k + 1) * C]

                dve.sem_inc(s["adj_free"], 1)
                dve.sem_inc(s["x_free"], 1)
                for q in range(2):
                    dve.sem_inc(s[f"rem_free{q}"], 1)
                    dve.sem_inc(s[f"key_counted{q}"], 1)
                    dve.sem_inc(s[f"key_stored{q}"], 16)
                dve.sem_inc(s["x1_stored"], 16)
                with dve.Fori(0, B) as b:
                    count[0] = 0
                    take(dve, "adj_for_dve")
                    for t in range(T):
                        done(v.scalar_tensor_tensor(out=nbkey[:, t, :], in0=adj_sb[:, t, :], scalar=0.0, in1=down[:],
                                                    op0=ALU.is_gt, op1=ALU.mult))
                        done(v.tensor_tensor(nbkey[:, t, bass.ts(t, P)], nbkey[:, t, bass.ts(t, P)], off_diag[:],
                                             ALU.mult))
                        done(v.tensor_scalar(nb[:], nbkey[:, t, :], 1.0, None, ALU.min))
                        done(v.tensor_tensor_scan(rank[:], ones_row[:], nb[:], 0.0, ALU.mult, ALU.add))
                        done(v.tensor_tensor(ranked[:, t, :], rank[:], nb[:], ALU.mult),
                             v.tensor_copy(nb_count[:, t:t + 1], rank[:, N - 1:N]))
                        if t == 1:
                            take(dve, "deg_ready")
                            done(v.tensor_scalar(safe_deg[:], deg[:], 1e-37, None, ALU.max),
                                 v.tensor_scalar(keep[:], deg[:], 0.0, None, ALU.not_equal),
                                 v.tensor_scalar(dsc[:], deg[:], 0.0, None, ALU.is_gt))
                            dve.sem_inc(s["safe_ready"], 1)
                        if t == 2:
                            take(dve, "pow_ready")
                            done(v.tensor_tensor(dsc[:], dsc[:], dpow[:], ALU.mult))
                            take(dve, "proj_ready")
                            start_product(order(3))
                        if t == 4:
                            apply_laplacian(order(3), order(2), 2.0, None, bb[0][:])
                            start_product(bb[0][:])
                        if t == 6:
                            apply_laplacian(bb[0][:], order(1), 2.0, order(3), bb[1][:])
                            start_product(bb[1][:])
                    dve.sem_inc(s["adj_free"], 1)
                    done(v.tensor_copy(count_i[:], nb_count[:]), v.tensor_copy(mask_b[:], mask_f[:, bass.ds(b * T, T)]),
                         v.tensor_scalar(dil[:], nb_count[:], float(T_THRESH), None, ALU.is_gt))
                    done(v.tensor_scalar(odd_i[:], count_i[:], 1, None, ALU.bitwise_and),
                         v.tensor_tensor(dil[:], dil[:], mask_b[:], ALU.mult))
                    done(v.tensor_copy(even[:], odd_i[:]), v.tensor_tensor(half_i[:], count_i[:], odd_i[:], ALU.add))
                    done(v.tensor_scalar(half_i[:], half_i[:], 1, None, ALU.logical_shift_right),
                         v.tensor_scalar(even[:], even[:], -1.0, 1.0, ALU.mult, ALU.add))
                    done(v.tensor_scalar(hit1[:], half_i[:], 1.0, None, ALU.add),
                         v.scalar_tensor_tensor(out=hit2[:], in0=nb_count[:], scalar=1.0, in1=even[:], op0=ALU.add,
                                                op1=ALU.mult))
                    done(v.tensor_tensor(hit1[:], hit1[:], dil[:], ALU.mult),
                         v.tensor_tensor(hit2[:], hit2[:], dil[:], ALU.mult))
                    done(v.tensor_scalar(hit1[:], hit1[:], -1.0, None, ALU.add),
                         v.tensor_scalar(hit2[:], hit2[:], -1.0, None, ALU.add))
                    for t in range(T):
                        done(v.tensor_scalar(first_hit[:], ranked[:, t, :], hit1[:, t:t + 1], None, ALU.is_equal))
                        done(v.scalar_tensor_tensor(out=removed[:, t, :], in0=ranked[:, t, :], scalar=hit2[:, t:t + 1],
                                                    in1=first_hit[:], op0=ALU.is_equal, op1=ALU.add))
                    dve.sem_inc(s["removed_ready"], 1)
                    done(v.tensor_tensor(tmp2[:], order(0), bb[0][:], ALU.subtract))
                    done(v.tensor_tensor(bb[2][:], tmp2[:], x_sb[:], ALU.add))
                    done(v.tensor_tensor(bb[2][:], bb[2][:], bias0_sb[:].unsqueeze(1).to_broadcast([P, T, C]),
                                         ALU.add))
                    dve.sem_inc(s["x_free"], 1)
                    apply_laplacian(bb[1][:], bb[2][:], 1.0, None, bb[0][:])
                    done(v.tensor_reduce(mean[:], bb[0][:], AX_X, ALU.add))
                    done(v.tensor_scalar(mean[:], mean[:], 1.0 / C, None, ALU.mult))
                    done(v.tensor_tensor(bb[1][:], bb[0][:], wide(mean[:]), ALU.subtract))
                    done(v.tensor_tensor(tmp[:], bb[1][:], bb[1][:], ALU.mult))
                    done(v.tensor_reduce(var[:], tmp[:], AX_X, ALU.add))
                    done(v.tensor_scalar(var[:], var[:], 1.0 / C, EPS, ALU.mult, ALU.add))
                    dve.sem_inc(s["var_ready"], 1)
                    for t in range(T):
                        q = t % 2
                        take(dve, f"rem_ready{q}")
                        take(dve, f"key_stored{q}", 16)
                        take(dve, f"key_counted{q}")
                        done(v.scalar_tensor_tensor(out=key_out[:, q, :], in0=rem_ps[q][:], scalar=0.0,
                                                    in1=nbkey[:, t, :], op0=ALU.is_equal, op1=ALU.mult))
                        dve.sem_inc(s[f"rem_free{q}"], 1)
                        done(v.tensor_tensor(key_out[:, q, bass.ts(t, P)], key_out[:, q, bass.ts(t, P)],
                                             diag_key[:, bass.ts(t, P)], ALU.add))
                        dve.sem_inc(s[f"key_ready{q}"], 1)
                        dve.sem_inc(s[f"key_for_act{q}"], 1)
                        if t == 1:
                            take(dve, "rstd_ready")
                            take(dve, "x1_stored", 16)
                            done(v.tensor_tensor(x1_sb[:], bb[1][:], wide(rstd[:]), ALU.mult))
                            dve.sem_inc(s["x1_ready"], 1)
                    dve.sem_clear(step)
                for q in range(2):
                    take(dve, f"key_stored{q}", 16)
                take(dve, "x1_stored", 16)

        with ExitStack() as bctx:
            def bsb(name, shape, dt):
                return bctx.enter_context(nc.sbuf_tensor(name, shape, dt))

            def bsem(name):
                return bctx.enter_context(nc.semaphore(name))

            NL = len(LEVELS)
            meta = bsb("meta", [P, COLS, META], F32)
            q_f = bsb("q_f", [P, COLS], F32)
            q_i = bsb("q_i", [P, COLS], I32)
            r_i = bsb("r_i", [P, COLS], I32)
            frac = bsb("frac", [P, COLS], F32)
            at_level = bsb("at_level", [P, NL, COLS], F32)
            above = bsb("above", [P, COLS], F32)
            ahead = bsb("ahead", [P, COLS], F32)
            colsum = bsb("colsum", [P, COLS], F32)
            place = bsb("place", [P, COLS], F32)
            place_i = bsb("place_i", [P, COLS], I32)
            total = bsb("total", [P, NL], F32)
            total_i = bsb("total_i", [P, NL], I32)
            node_i = bsb("node_i", [P, COLS], I32)
            node_p = bsb("node_p", [P, COLS], I32)
            pads = bsb("pads", [P, NL * LIST // P], I32)
            pad_meta = bsb("pad_meta", [P, META], F32)
            count_ps = bctx.enter_context(nc.psum_tensor("count_ps", [P, 2, 512], F32))
            records_ready, nodes_ready, counted, level_ready, places_ready, pads_ready, pads_stored, stored, listed = (
                bsem(n) for n in ("records_ready", "nodes_ready", "counted", "level_ready", "places_ready",
                                  "pads_ready", "pads_stored", "records_stored", "listed"))
            block = bctx.enter_context(nc.Block())

            @block.sync
            def _(sp):
                sp.wait_ge(pads_ready, 1)
                sp.dma_start(lists.rearrange("(p k) o -> p (k o)", p=P), pads[:]).then_inc(pads_stored, 16)
                sp.dma_start(rows(meta_rows, NODES, P), pad_meta[:]).then_inc(stored, 16)
                sp.wait_ge(records_ready, 1)
                sp.dma_start(rows(meta_rows, 0, NODES).rearrange("(c p) k -> p c k", p=P), meta[:]).then_inc(stored, 16)
                sp.wait_ge(stored, 32)

            @block.gpsimd
            def _(pool):
                nc.gpsimd.iota(node_i[:], pattern=[[P, COLS]], base=0, channel_multiplier=1).then_inc(nodes_ready, 1)
                pool.wait_ge(nodes_ready, 1)
                pool.wait_ge(pads_stored, 16)
                pool.wait_ge(places_ready, 1)
                for c in range(COLS):
                    pool.indirect_dma_start(lists, bass.IndirectOffsetOnAxis(ap=place_i[:, c:c + 1].bitcast(U32), axis=0),
                                            node_i[:, c:c + 1], None).then_inc(listed, 16)
                pool.wait_ge(listed, 16 * COLS)

            @block.tensor
            def _(pe):
                pe.wait_ge(level_ready, 1)
                for g in range(2):
                    lhs = (before, ones)[g]
                    mm = nc.tensor.matmul(count_ps[:, g, 0:NL * COLS], lhs[:],
                                          at_level[:].rearrange("p l c -> p (l c)"), start=True, stop=True)
                mm.then_inc(counted, 1)

            @block.vector
            def _(dve):
                v = nc.vector
                count = [0]

                def done(*instructions):
                    for i in instructions:
                        i.then_inc(step, 1)
                    count[0] += len(instructions)
                    dve.wait_ge(step, count[0])

                done(v.memset(pads[:], NODES), v.memset(pad_meta[:], 0.0), v.memset(meta[:], 0.0))
                done(v.memset(pad_meta[:, 10:11], float(NODES)))
                dve.sem_inc(pads_ready, 1)
                for i, (tau, wt) in enumerate(zip(TAUS, QWEIGHTS)):
                    done(v.tensor_scalar(q_f[:], m_all[:], -1.0, tau * 4, ALU.add, ALU.mult))
                    done(v.tensor_copy(q_i[:], q_f[:]))
                    done(v.tensor_scalar(r_i[:], q_i[:], 3, None, ALU.bitwise_and))
                    done(v.tensor_scalar(q_i[:], q_i[:], 2, None, ALU.logical_shift_right))
                    done(v.tensor_copy(meta[:, :, i], q_i[:]), v.tensor_scalar(frac[:], r_i[:], 0.25, None, ALU.mult))
                    done(v.tensor_scalar(meta[:, :, 3 + i], frac[:], -wt, wt, ALU.mult, ALU.add),
                         v.tensor_scalar(meta[:, :, 6 + i], frac[:], wt, None, ALU.mult))
                dve.wait_ge(nodes_ready, 1)
                shift = N.bit_length() - 1
                done(v.tensor_scalar(node_p[:], node_i[:], shift, shift, ALU.logical_shift_right,
                                     ALU.logical_shift_left))
                done(v.tensor_scalar(meta[:, :, 9], node_p[:], float(N), None, ALU.add),
                     v.tensor_scalar(meta[:, :, 10], node_p[:], -1.0, float(NODES - N), ALU.mult, ALU.add))
                dve.sem_inc(records_ready, 1)
                low = 0
                for i, cap in enumerate(LEVELS):
                    done(v.tensor_scalar(above[:], m_all[:], float(low), None, ALU.is_gt))
                    done(v.scalar_tensor_tensor(out=at_level[:, i, :], in0=m_all[:], scalar=float(cap), in1=above[:],
                                                op0=ALU.is_le, op1=ALU.mult))
                    low = cap
                dve.sem_inc(level_ready, 1)
                dve.wait_ge(counted, 1)
                for i, cap in enumerate(LEVELS):
                    done(v.tensor_copy(colsum[:], count_ps[:, 1, bass.ts(i, COLS)]))
                    done(v.tensor_tensor_scan(ahead[:], ones[:, 0:COLS], colsum[:], 0.0, ALU.mult, ALU.add))
                    done(v.tensor_copy(total[:, i:i + 1], ahead[:, COLS - 1:COLS]),
                         v.tensor_tensor(colsum[:], ahead[:], colsum[:], ALU.subtract))
                    done(v.tensor_tensor(colsum[:], colsum[:], count_ps[:, 0, bass.ts(i, COLS)], ALU.add))
                    done(v.scalar_tensor_tensor(out=colsum[:], in0=colsum[:], scalar=float(i * LIST),
                                                in1=at_level[:, i, :], op0=ALU.add, op1=ALU.mult))
                    if i == 0:
                        done(v.tensor_copy(place[:], colsum[:]))
                    else:
                        done(v.tensor_tensor(place[:], place[:], colsum[:], ALU.add))
                    size = P if cap in WIDE else NARROW_NODES
                    done(v.tensor_scalar(total[:, i:i + 1], total[:, i:i + 1], float(size - 1), None, ALU.add))
                done(v.tensor_copy(place_i[:], place[:]), v.tensor_copy(total_i[:], total[:]))
                dve.sem_inc(places_ready, 1)
                for first, last, size in ((0, len(WIDE), P), (len(WIDE), NL, NARROW_NODES)):
                    done(v.tensor_scalar(tiles_of[:, first:last], total_i[:, first:last], size.bit_length() - 1, None,
                                         ALU.logical_shift_right))
                dve.sem_clear(step)

        with ExitStack() as cctx:
            def csb(name, shape, dt):
                return cctx.enter_context(nc.sbuf_tensor(name, shape, dt))

            def csem(name):
                return cctx.enter_context(nc.semaphore(name))

            ids = csb("ids", [P, 1], I32)
            out_ids = csb("out_ids", [P, 1], I32)
            keys = csb("keys", [P, N], F16)
            record = csb("record", [P, META], F32)
            record2 = csb("record2", [P, META], F32)
            found = csb("found", [P, BLOCK], F32)
            unused = csb("unused", [P, BLOCK], F32)
            nbr_f = csb("nbr_f", [P, BLOCK], F32)
            nbr_i = csb("nbr_i", [P, BLOCK], I32)
            stage = csb("stage", [P, BLOCK, C // GROUPS], F32)
            weight = csb("weight", [P, N], F32)
            agg = csb("agg", [P, C], F32)
            ids_free, ids_loaded, tile_loaded, tile_ready, nbr_ready, gathered_dma, gathered, agg_ready, agg_stored = (
                csem(n) for n in ("ids_free", "ids_loaded", "tile_loaded", "tile_ready", "nbr_ready", "gathered_dma",
                                  "gathered", "agg_ready", "agg_stored"))
            block = cctx.enter_context(nc.Block())

            def get(eng, semaphore, n=1):
                eng.wait_ge(semaphore, n)
                eng.sem_clear(semaphore)

            def each_tile(eng, level, body):
                cap = LEVELS[level]
                n = eng.value_load(tiles_of[0:1, level:level + 1], min_val=0, max_val=NODES // NARROW_NODES)
                if cap in WIDE:
                    with eng.Fori(0, NODES // P) as i:
                        with eng.If(i < n):
                            body(i)
                        with eng.Else():
                            eng.nop()
                        eng.nop()
                    return
                inner = 16
                with eng.Fori(0, NODES // NARROW_NODES // inner) as o:
                    with eng.If(o * inner < n):
                        with eng.Fori(0, inner) as i:
                            with eng.If(o * inner + i < n):
                                body(o * inner + i)
                            with eng.Else():
                                eng.nop()
                            eng.nop()
                        eng.nop()
                    with eng.Else():
                        eng.nop()
                    eng.nop()

            @block.sync
            def _(sp):
                for level, cap in enumerate(LEVELS):
                    def load_ids(i):
                        get(sp, ids_free)
                        if cap in WIDE:
                            sp.dma_start(ids[:], lists[bass.ds(i * P + level * LIST, P)]).then_inc(ids_loaded, 16)
                            sp.wait_ge(ids_loaded, 16)
                        else:
                            for g in range(GROUPS):
                                sp.dma_start(ids[bass.ts(g, NARROW_NODES), :],
                                             lists[bass.ds(i * NARROW_NODES + level * LIST, NARROW_NODES)]).then_inc(
                                    ids_loaded, 16)
                            sp.wait_ge(ids_loaded, 16 * GROUPS)
                        sp.sem_clear(ids_loaded)
                        sp.sem_inc(tile_loaded, 1)
                    each_tile(sp, level, load_ids)

            @block.gpsimd
            def _(pool):
                pool.sem_inc(ids_free, 1)
                for level, cap in enumerate(LEVELS):
                    wide_level = cap in WIDE

                    def gather_block(cap=cap, wide_level=wide_level):
                        get(pool, nbr_ready)
                        for k in range(min(cap, BLOCK)):
                            where = bass.IndirectOffsetOnAxis(ap=nbr_i[:, k:k + 1].bitcast(U32), axis=0)
                            if wide_level:
                                dst, src = slots[0][:, k * C:(k + 1) * C], x1_rows
                            else:
                                dst, src = stage[:, k, :], x1_rows.rearrange("n (g c) -> (n g) c", g=GROUPS)
                            pool.indirect_dma_start(dst, None, src, where).then_inc(gathered_dma, 16)
                        pool.drain().then_inc(gathered, 1)

                    def tile(i, cap=cap, wide_level=wide_level):
                        get(pool, tile_loaded)
                        where = bass.IndirectOffsetOnAxis(ap=ids[:].bitcast(U32), axis=0)
                        pool.indirect_dma_start(keys[:], None, key_rows, where).then_inc(gathered_dma, 16)
                        pool.indirect_dma_start(record[:], None, meta_rows, where).then_inc(gathered_dma, 16)
                        pool.drain().then_inc(tile_ready, 1)
                        if cap <= BLOCK:
                            gather_block()
                        else:
                            with pool.Fori(0, cap // BLOCK):
                                gather_block()
                        get(pool, agg_ready)
                        if wide_level:
                            pool.indirect_dma_start(agg_rows,
                                                    bass.IndirectOffsetOnAxis(ap=out_ids[:].bitcast(U32), axis=0),
                                                    agg[:], None, bounds_check=NODES - 1,
                                                    oob_is_err=False).then_inc(agg_stored, 16)
                        else:
                            pool.indirect_dma_start(agg_rows.rearrange("n (g c) -> (n g) c", g=GROUPS),
                                                    bass.IndirectOffsetOnAxis(ap=out_ids[:].bitcast(U32), axis=0),
                                                    agg[:, 0:C // GROUPS], None, bounds_check=NODES * GROUPS - 1,
                                                    oob_is_err=False).then_inc(agg_stored, 16)
                        pool.drain().then_inc(ids_free, 1)
                    each_tile(pool, level, tile)

            @block.vector
            def _(dve):
                v = nc.vector
                count = [0]

                def done(*instructions):
                    for i in instructions:
                        i.then_inc(step, 1)
                    count[0] += len(instructions)
                    dve.wait_ge(step, count[0])

                def restart():
                    dve.sem_clear(step)
                    count[0] = 0

                def find_neighbours(n, wide_level):
                    for r in range(n // 8):
                        done(v.max(found[:, bass.ts(r, 8)], keys[:]))
                        done(v.match_replace(keys[:], found[:, bass.ts(r, 8)], keys[:], 0.0))
                    f = found[:, 0:n]
                    done(v.tensor_scalar(unused[:, 0:n], f, 0.0, record2[:, 10:11], ALU.is_equal, ALU.mult))
                    done(v.tensor_scalar(nbr_f[:, 0:n], f, -1.0, record2[:, 9:10], ALU.mult, ALU.add))
                    if wide_level:
                        done(v.tensor_tensor(nbr_i[:, 0:n], nbr_f[:, 0:n], unused[:, 0:n], ALU.add))
                    else:
                        done(v.tensor_tensor(nbr_f[:, 0:n], nbr_f[:, 0:n], unused[:, 0:n], ALU.add))
                        done(v.tensor_scalar(nbr_i[:, 0:n], nbr_f[:, 0:n], float(GROUPS), group_f[:, 0:1], ALU.mult,
                                             ALU.add))
                    dve.sem_inc(nbr_ready, 1)

                def sort(cap, width):
                    src, dst = 0, 1
                    for p, k in sort_stages(cap):
                        a = slots[src][:, 0:cap * width].rearrange("q (b w) -> q b w", w=2 * p * width)
                        z = slots[dst][:, 0:cap * width].rearrange("q (b w) -> q b w", w=2 * p * width)
                        edge = 0 if k == p else k * width
                        body = slice(edge, 2 * p * width - edge)
                        pa = a[:, :, body].rearrange("q b (g two w) -> q b g two w", two=2, w=k * width)
                        pz = z[:, :, body].rearrange("q b (g two w) -> q b g two w", two=2, w=k * width)
                        ops = [v.tensor_tensor(pz[:, :, :, 0, :], pa[:, :, :, 0, :], pa[:, :, :, 1, :], ALU.min),
                               v.tensor_tensor(pz[:, :, :, 1, :], pa[:, :, :, 0, :], pa[:, :, :, 1, :], ALU.max)]
                        if edge:
                            ops += [v.tensor_copy(z[:, :, 0:edge], a[:, :, 0:edge]),
                                    v.tensor_copy(z[:, :, 2 * p * width - edge:], a[:, :, 2 * p * width - edge:])]
                        done(*ops)
                        src, dst = dst, src
                    return src

                for level, cap in enumerate(LEVELS):
                    wide_level = cap in WIDE
                    width = C if wide_level else C // GROUPS

                    def tile(i, cap=cap, wide_level=wide_level, width=width):
                        get(dve, tile_ready)
                        done(v.tensor_copy(record2[:], record[:]),
                             v.tensor_copy(out_ids[:], ids[:]) if wide_level else
                             v.tensor_scalar(out_ids[:], ids[:], float(GROUPS), group_f[:, 0:1], ALU.mult, ALU.add))
                        if cap <= BLOCK:
                            find_neighbours(cap, wide_level)
                            get(dve, gathered)
                        else:
                            restart()
                            with dve.Fori(0, cap // BLOCK) as blk:
                                find_neighbours(BLOCK, wide_level)
                                get(dve, gathered)
                                done(v.tensor_copy(slots[0][:, bass.ds(blk * (BLOCK * width), BLOCK * width)],
                                                   stage[:].rearrange("p k c -> p (k c)")))
                                restart()
                        at = sort(cap, width)
                        done(v.memset(weight[:, 0:cap], 0.0))
                        for q in range(len(TAUS)):
                            for ahead_by, col in ((0, 3), (1, 6)):
                                done(v.tensor_scalar(slots[1 - at][:, 0:cap], up[:, 0:cap], float(-ahead_by),
                                                     record2[:, q:q + 1], ALU.add, ALU.is_equal))
                                done(v.scalar_tensor_tensor(out=weight[:, 0:cap], in0=slots[1 - at][:, 0:cap],
                                                            scalar=record2[:, col + q:col + q + 1],
                                                            in1=weight[:, 0:cap], op0=ALU.mult, op1=ALU.add))
                        done(v.tensor_tensor(slots[1 - at][:, 0:cap * width].rearrange("p (k c) -> p k c", c=width),
                                             slots[at][:, 0:cap * width].rearrange("p (k c) -> p k c", c=width),
                                             weight[:, 0:cap].unsqueeze(2).to_broadcast([P, cap, width]), ALU.mult))
                        done(v.tensor_reduce(agg[:, 0:width],
                                             slots[1 - at][:, 0:cap * width].rearrange("p (k c) -> p c k", c=width),
                                             AX_X, ALU.add))
                        dve.sem_inc(agg_ready, 1)
                        restart()
                    each_tile(dve, level, tile)

        with ExitStack() as dctx:
            def dsb(name, shape, dt):
                return dctx.enter_context(nc.sbuf_tensor(name, shape, dt))

            def dsem(name):
                return dctx.enter_context(nc.semaphore(name))

            x1_in = [dsb(f"x1_in{i}", [P, T, C], F32) for i in range(2)]
            agg_in = [dsb(f"agg_in{i}", [P, T, C], F32) for i in range(2)]
            res = dsb("res", [P, T, C], F32)
            resT = dsb("resT", [C, N], F32)
            hidT = dsb("hidT", [H, N], F32)
            y = dsb("y", [P, T, C], F32)
            cen = dsb("cen", [P, T, C], F32)
            sq = dsb("sq", [P, T, C], F32)
            mean = dsb("mean_d", [P, T], F32)
            var = dsb("var_d", [P, T], F32)
            rstd = dsb("rstd_d", [P, T], F32)
            fin = [dsb(f"fin{i}", [P, T, C], F32) for i in range(2)]
            resT_ps = dctx.enter_context(nc.psum_tensor("resT_ps", [C, N], F32))
            hid_ps = dctx.enter_context(nc.psum_tensor("hid_ps", [H, N], F32))
            out_ps = dctx.enter_context(nc.psum_tensor("out_ps", [P, T, C], F32))
            in_loaded = [dsem(f"in_loaded{i}") for i in range(2)]
            fin_stored = [dsem(f"fin_stored{i}") for i in range(2)]
            in_used, res_ready, resT_ready, resT_copied, hid_ready, hid_act, out_ready, y_done, var_ready, rstd_ready, fin_ready = (
                dsem(n) for n in ("in_used", "res_ready", "resT_ready", "resT_copied", "hid_ready", "hid_act",
                                  "out_ready", "y_done", "var_ready_d", "rstd_ready_d", "fin_ready"))
            block = dctx.enter_context(nc.Block())

            @block.sync
            def _(sp):
                def load(b):
                    for dst, src in ((x1_in, x1_rows), (agg_in, agg_rows)):
                        sp.dma_start(dst[b % 2][:], src[b * N:(b + 1) * N, :].rearrange("(t p) c -> p t c", p=P)).then_inc(
                            in_loaded[b % 2], 16)

                load(0)
                for b in range(B):
                    if b + 1 < B:
                        if b >= 1:
                            sp.wait_ge(in_used, b)
                        load(b + 1)
                    sp.wait_ge(fin_ready, b + 1)
                    sp.dma_start(out[b].rearrange("(t p) c -> p t c", p=P), fin[b % 2][:]).then_inc(fin_stored[b % 2], 16)
                for q in range(2):
                    sp.wait_ge(fin_stored[q], 16 * (B // 2))

            @block.tensor
            def _(pe):
                for b in range(B):
                    pe.wait_ge(res_ready, b + 1)
                    for t in range(T):
                        mm = nc.tensor.transpose(resT_ps[:, bass.ts(t, P)], res[:, t, :], ident[:])
                    mm.then_inc(resT_ready, 1)
                    pe.wait_ge(resT_copied, b + 1)
                    for h in range(2):
                        mm = nc.tensor.matmul(hid_ps[:, bass.ts(h, 512)], W1_sb[:], resT[:, bass.ts(h, 512)],
                                              start=True, stop=True)
                    mm.then_inc(hid_ready, 1)
                    pe.wait_ge(hid_act, b + 1)
                    if b:
                        pe.wait_ge(y_done, b)
                    for t in range(T):
                        mm = nc.tensor.matmul(out_ps[:, t, :], hidT[:, bass.ts(t, P)], W2_sb[:], start=True, stop=True)
                    mm.then_inc(out_ready, 1)

            @block.scalar
            def _(act):
                for b in range(B):
                    act.wait_ge(resT_ready, b + 1)
                    nc.scalar.copy(resT[:], resT_ps[:]).then_inc(resT_copied, 1)
                    act.wait_ge(hid_ready, b + 1)
                    nc.scalar.activation(hidT[:], hid_ps[:], ACT.Relu, bias=b1_sb[:, 0:1]).then_inc(hid_act, 1)

            @block.gpsimd
            def _(pool):
                for b in range(B):
                    pool.wait_ge(var_ready, b + 1)
                    nc.gpsimd.tensor_tensor(rstd[:], var[:], power[:], ALU.pow).then_inc(rstd_ready, 1)

            @block.vector
            def _(dve):
                v = nc.vector
                count = [0]

                def done(*instructions):
                    for i in instructions:
                        i.then_inc(step, 1)
                    count[0] += len(instructions)
                    dve.wait_ge(step, count[0])

                def wide(ap):
                    return ap.unsqueeze(2).to_broadcast([P, T, C])

                def make_res(b):
                    dve.wait_ge(in_loaded[b % 2], 32 * (b // 2 + 1))
                    if b:
                        dve.wait_ge(resT_ready, b)
                    done(v.tensor_tensor(res[:], x1_in[b % 2][:], agg_in[b % 2][:], ALU.add))
                    dve.sem_inc(res_ready, 1)

                make_res(0)
                for b in range(B):
                    dve.wait_ge(out_ready, b + 1)
                    done(v.tensor_tensor(y[:], out_ps[:], b2_sb[:].unsqueeze(1).to_broadcast([P, T, C]), ALU.add))
                    dve.sem_inc(y_done, 1)
                    if b + 1 < B:
                        make_res(b + 1)
                    done(v.tensor_tensor(y[:], y[:], wide(mask_f[:, b * T:(b + 1) * T]), ALU.mult))
                    done(v.tensor_tensor(y[:], y[:], x1_in[b % 2][:], ALU.add))
                    dve.sem_inc(in_used, 1)
                    done(v.tensor_reduce(mean[:], y[:], AX_X, ALU.add))
                    done(v.tensor_scalar(mean[:], mean[:], 1.0 / C, None, ALU.mult))
                    done(v.tensor_tensor(cen[:], y[:], wide(mean[:]), ALU.subtract))
                    done(v.tensor_tensor(sq[:], cen[:], cen[:], ALU.mult))
                    done(v.tensor_reduce(var[:], sq[:], AX_X, ALU.add))
                    done(v.tensor_scalar(var[:], var[:], 1.0 / C, EPS, ALU.mult, ALU.add))
                    dve.sem_inc(var_ready, 1)
                    dve.wait_ge(rstd_ready, b + 1)
                    if b >= 2:
                        dve.wait_ge(fin_stored[b % 2], 16 * (b // 2))
                    done(v.tensor_tensor(fin[b % 2][:], cen[:], wide(rstd[:]), ALU.mult))
                    dve.sem_inc(fin_ready, 1)


def kernel(x, adj, nodemask, L0_gnn_weight, L0_gnn_bias, L1_gnn_W1, L1_gnn_b1, L1_gnn_W2, L1_gnn_b2):
    import numpy as np
    import concourse.bacc as bacc
    from concourse.bass_utils import run_bass_kernel_spmd

    x = np.asarray(x)
    adj = np.asarray(adj)
    mask = np.asarray(nodemask).view(np.uint8)
    w0 = np.asarray(L0_gnn_weight)
    C = x.shape[2]
    data = {
        "x": x,
        "xT": x.transpose(0, 2, 1),
        "adj": adj,
        "adjT": adj.transpose(0, 2, 1),
        "mask": mask.reshape(-1, P).T,
        "w_cat": w0[:, 0].transpose(1, 0, 2).reshape(C, -1),
        "bias0": np.asarray(L0_gnn_bias).reshape(-1),
        "W1": np.asarray(L1_gnn_W1),
        "b1": np.asarray(L1_gnn_b1).reshape(-1, 1),
        "W2": np.asarray(L1_gnn_W2),
        "b2": np.asarray(L1_gnn_b2).reshape(-1),
    }
    data = {f"in_{k}": np.ascontiguousarray(a) for k, a in data.items()}
    nc = bacc.Bacc("TRN2", target_bir_lowering=False, num_devices=1)
    args = [nc.dram_tensor(k, a.shape, mybir.dt.from_np(a.dtype), kind="ExternalInput").ap() for k, a in data.items()]
    out = nc.dram_tensor("out", x.shape, F32, kind="ExternalOutput").ap()
    build(nc, *args, out)
    result = run_bass_kernel_spmd(nc, [data], core_ids=[0])
    return result.results[0]["out"]
```

```python
from contextlib import ExitStack

import concourse.bass as bass
from concourse import mybir

F32 = mybir.dt.float32
F16 = mybir.dt.float16
BF16 = mybir.dt.bfloat16
I32 = mybir.dt.int32
U32 = mybir.dt.uint32
U8 = mybir.dt.uint8
ALU = mybir.AluOpType
ACT = mybir.ActivationFunctionType
AX_X = mybir.AxisListType.X

P = 128
EPS = 1e-5
T_THRESH = 10
TAUS = (0.25, 0.5, 0.75)
QWEIGHTS = (0.25, 0.5, 0.25)
PAD_VALUE = 1e30
WIDE = (8, 12, 16, 20, 24, 32, 48, 64, 128)
NARROW = {256: 4, 512: 8, 1024: 8}
LEVELS = WIDE + tuple(NARROW)
BLOCK = 64
META = 16
LOWER, W_LOW, W_UP, FIRST, TO_PAD, NODE = 0, 3, 6, 9, 10, 11


def sort_stages(n):
    p = 1
    while p < n:
        k = p
        while k >= 1:
            yield p, k
            k //= 2
        p *= 2


def stage_parts(n, p, k):
    block = 2 * p
    full, rest = divmod(n, block)
    edge = 0 if k == p else k
    compared, kept = [], []
    if full:
        compared.append((edge, block, full, (block - 2 * edge) // (2 * k), k))
        if edge:
            kept += [(0, block, full, edge), (block - edge, block, full, edge)]
    if rest:
        start = full * block
        groups = max(0, (rest - edge) // (2 * k))
        if k == p:
            groups = 0
        at = edge + groups * 2 * k
        tail = max(0, rest - at - k)
        if groups:
            compared.append((start + edge, block, 1, groups, k))
        if tail:
            compared.append((start + at, block, 1, 1, tail))
        if edge:
            kept.append((start, block, 1, min(edge, rest)))
        if at + tail < min(at + k, rest):
            kept.append((start + at + tail, block, 1, min(at + k, rest) - at - tail))
    return compared, kept


def build(nc, x, xT, adj, adjT, mask, w_cat, bias0, W1, b1, W2, b2, out):
    B, N, C = x.shape
    H = W1.shape[1]
    T = N // P
    NODES = B * N
    COLS = NODES // P
    LIST = NODES + P
    K0 = w_cat.shape[1] // C

    ROW = N + 2 * META
    TILES = NODES // P + len(WIDE) + 3
    TABLE = P * TILES
    key_rows = nc.dram_tensor("key_rows", (NODES + 1, ROW), F16, kind="Internal").ap()
    x1_rows = nc.dram_tensor("x1_rows", (NODES + 1, C), F32, kind="Internal").ap()
    agg_rows = nc.dram_tensor("agg_rows", (NODES, C), F32, kind="Internal").ap()
    lists = nc.dram_tensor("lists", (TABLE + len(NARROW) * LIST, 1), I32, kind="Internal").ap()

    with ExitStack() as ctx:
        def sb(name, shape, dt):
            return ctx.enter_context(nc.sbuf_tensor(name, shape, dt))

        def ps(name, shape, dt=F32):
            return ctx.enter_context(nc.psum_tensor(name, shape, dt))

        def sem(name):
            return ctx.enter_context(nc.semaphore(name))

        diff = sb("diff", [P, P], I32)
        ident = sb("ident", [P, P], F32)
        ident_b = sb("ident_b", [P, P], BF16)
        off_diag = sb("off_diag", [P, P], F16)
        before = sb("before", [P, P], F32)
        ones = sb("ones", [P, P], F32)
        ramp_i = sb("ramp_i", [P, N], I32)
        down = sb("down", [P, N], F16)
        up = sb("up", [P, N], F32)
        diag_key = sb("diag_key", [P, N], F16)
        ones_row = sb("ones_row", [P, N], F16)
        part_i = sb("part_i", [P, 1], I32)
        group_f = {g: sb(f"group_f{g}", [P, 1], F32) for g in sorted(set(NARROW.values()))}
        group_i = {g: sb(f"group_i{g}", [P, 1], I32) for g in group_f}
        up_less = sb("up_less", [P, N], F32)
        eps_t = sb("eps_t", [P, T], F32)
        power = sb("power", [P, T], F32)
        wcat_sb = sb("wcat_sb", [C, K0 * C], F32)
        bias0_sb = sb("bias0_sb", [P, C], F32)
        W1_sb = sb("W1_sb", [C, H], F32)
        b1_sb = sb("b1_sb", [H, 1], F32)
        W2_sb = sb("W2_sb", [H, C], F32)
        b2_sb = sb("b2_sb", [P, C], F32)
        mask_u = sb("mask_u", [P, COLS], U8)
        mask_f = sb("mask_f", [P, COLS], F32)
        m_all = sb("m_all", [P, COLS], F32)
        tiles_of = sb("tiles_of", [P, len(LEVELS) + 1], I32)

        slots = [sb(f"slots{i}", [P, T * N], F32) for i in range(2)]

        def rows(ap, first, n):
            return ap[first:first + n, :]

        step = sem("step")

        with ExitStack() as sctx:
            loaded = sctx.enter_context(nc.semaphore("weights_loaded"))
            iotas = sctx.enter_context(nc.semaphore("iotas_done"))
            consts = sctx.enter_context(nc.semaphore("consts_done"))
            pad_stored = sctx.enter_context(nc.semaphore("pad_stored"))
            pad_f = sctx.enter_context(nc.sbuf_tensor("pad_f", [1, C], F32))
            pad_k = sctx.enter_context(nc.sbuf_tensor("pad_k", [1, ROW], F16))
            pad_meta = pad_k[:, N:ROW].bitcast(F32)
            block = sctx.enter_context(nc.Block())

            @block.sync
            def _(sp):
                sp.dma_start(wcat_sb[:], w_cat).then_inc(loaded, 16)
                sp.dma_start(bias0_sb[:], bias0.partition_broadcast(P)).then_inc(loaded, 16)
                sp.dma_start(W1_sb[:], W1).then_inc(loaded, 16)
                sp.dma_start(b1_sb[:], b1).then_inc(loaded, 16)
                sp.dma_start(W2_sb[:], W2).then_inc(loaded, 16)
                sp.dma_start(b2_sb[:], b2.partition_broadcast(P)).then_inc(loaded, 16)
                sp.dma_start(mask_u[:], mask).then_inc(loaded, 16)
                sp.wait_ge(consts, 1)
                sp.dma_start(rows(x1_rows, NODES, 1), pad_f[:]).then_inc(pad_stored, 16)
                sp.dma_start(rows(key_rows, NODES, 1), pad_k[:]).then_inc(pad_stored, 16)
                sp.wait_ge(pad_stored, 32)
                sp.wait_ge(loaded, 16 * 7)

            @block.gpsimd
            def _(pool):
                nc.gpsimd.iota(diff[:], pattern=[[1, P]], base=0, channel_multiplier=-1).then_inc(iotas, 1)
                nc.gpsimd.iota(ramp_i[:], pattern=[[1, N]], base=0, channel_multiplier=0).then_inc(iotas, 1)
                nc.gpsimd.iota(part_i[:], pattern=[[0, 1]], base=0, channel_multiplier=1).then_inc(iotas, 1)

            @block.vector
            def _(dve):
                count = [0]

                def done(*instructions):
                    for i in instructions:
                        i.then_inc(step, 1)
                    count[0] += len(instructions)
                    dve.wait_ge(step, count[0])

                dve.wait_ge(iotas, 3)
                dve.wait_ge(loaded, 16 * 7)
                v = nc.vector
                done(
                    v.tensor_scalar(ident[:], diff[:], 0, None, ALU.is_equal),
                    v.tensor_scalar(ident_b[:], diff[:], 0, None, ALU.is_equal),
                    v.tensor_scalar(off_diag[:], diff[:], 0, None, ALU.not_equal),
                    v.tensor_scalar(before[:], diff[:], 0, None, ALU.is_gt),
                    v.memset(ones[:], 1.0),
                    v.memset(ones_row[:], 1.0),
                    v.memset(eps_t[:], EPS),
                    v.memset(power[:], -0.5),
                    v.memset(pad_f[:], PAD_VALUE),
                    v.memset(pad_k[:], 0.0),
                    v.tensor_scalar(down[:], ramp_i[:], -1.0, float(N), ALU.mult, ALU.add),
                    v.tensor_copy(up[:], ramp_i[:]),
                    v.tensor_scalar(up_less[:], ramp_i[:], -1.0, None, ALU.add),
                    *[v.tensor_scalar(group_i[g][:], part_i[:], (P // g).bit_length() - 1, None,
                                      ALU.logical_shift_right) for g in group_i],
                    v.tensor_copy(mask_f[:], mask_u[:]),
                )
                done(*[v.tensor_copy(group_f[g][:], group_i[g][:]) for g in group_i],
                     v.memset(pad_meta[:, TO_PAD:TO_PAD + 1], float(NODES)),
                     v.memset(pad_meta[:, NODE:NODE + 1], float(NODES)),
                     *[v.tensor_tensor(diag_key[:, bass.ts(t, P)], down[:, bass.ts(t, P)], ident_b[:], ALU.mult)
                       for t in range(T)])
                dve.sem_inc(consts, 1)
                dve.sem_clear(step)

        with ExitStack() as actx:
            def asb(name, shape, dt):
                return actx.enter_context(nc.sbuf_tensor(name, shape, dt))

            def asem(name):
                return actx.enter_context(nc.semaphore(name))

            adj_sb = slots[0][:].rearrange("p (t n) -> p t n", t=T)
            adjT_sb = slots[1][:].rearrange("p (t n) -> p t n", t=T)
            x_sb = asb("x_sb", [P, T, C], F32)
            xT_sb = asb("xT_sb", [C, N], F32)
            nbkey = asb("nbkey", [P, T, N], F16)
            ranked = asb("ranked", [P, T, N], F16)
            removed = asb("removed", [P, T, N], BF16)
            nb = asb("nb", [P, N], F16)
            rank = asb("rank", [P, N], F16)
            first_hit = asb("first_hit", [P, N], BF16)
            key_out = asb("key_out", [P, 2, N], F16)
            act_junk = asb("act_junk", [P, N], BF16)
            deg = asb("deg", [P, T], F32)
            safe_deg = asb("safe_deg", [P, T], F32)
            dpow = asb("dpow", [P, T], F32)
            dsc = asb("dsc", [P, T], F32)
            keep = asb("keep", [P, T], F32)
            m_batch = asb("m_batch", [P, T], F32)
            nb_count = asb("nb_count", [P, T], F32)
            count_i = asb("count_i", [P, T], I32)
            half_i = asb("half_i", [P, T], I32)
            odd_i = asb("odd_i", [P, T], I32)
            hit1 = asb("hit1", [P, T], F32)
            hit2 = asb("hit2", [P, T], F32)
            dil = asb("dil", [P, T], F32)
            mask_b = asb("mask_b", [P, T], F32)
            even = asb("even", [P, T], F32)
            proj = asb("proj", [P, T, K0 * C], F32)
            z = asb("z", [P, T, C], F32)
            bb = [asb(f"bb{i}", [P, T, C], F32) for i in range(3)]
            tmp = asb("tmp", [P, T, C], F32)
            tmp2 = asb("tmp2", [P, T, C], F32)
            mean = asb("mean", [P, T], F32)
            var = asb("var", [P, T], F32)
            rstd = asb("rstd", [P, T], F32)
            x1_sb = asb("x1_sb", [P, T, C], F32)

            proj_ps = actx.enter_context(nc.psum_tensor("proj_ps", [P, T // 2, K0 * C], F32))
            y_ps = actx.enter_context(nc.psum_tensor("y_ps", [P, T, C], F32))
            rem_ps = [actx.enter_context(nc.psum_tensor(f"rem_ps{i}", [P, N], F32)) for i in range(2)]

            names = ("adj_loaded adjT_loaded x_loaded adj_for_dve adj_for_act adj_free adjT_free x_free "
                     "deg_ready pow_ready safe_ready var_ready rstd_ready half_projected half_copied proj_ready z_ready y_ready "
                     "removed_ready rem_ready0 rem_ready1 rem_free0 rem_free1 key_ready0 key_ready1 key_for_act0 "
                     "key_for_act1 key_counted0 key_counted1 key_stored0 key_stored1 x1_ready x1_stored m_ready").split()
            s = {n: asem(n) for n in names}
            astep = asem("astep")
            astep_pe = asem("astep_pe")
            block = actx.enter_context(nc.Block())

            def take(eng, name, n=1):
                eng.wait_ge(s[name], n)
                eng.sem_clear(s[name])

            @block.sync
            def _(sp):
                with sp.Fori(0, B) as b:
                    take(sp, "adj_free", 2)
                    sp.dma_start(adj_sb, adj[bass.ds(b, 1)].rearrange("o (t p) n -> p (o t) n", p=P)).then_inc(
                        s["adj_loaded"], 16)
                    take(sp, "x_free", 2)
                    xr = x[bass.ds(b, 1)].rearrange("o (t p) c -> p (o t) c", p=P)
                    sp.dma_start(x_sb[:], xr).then_inc(s["x_loaded"], 16)
                    sp.dma_start(xT_sb[:], xT[bass.ds(b, 1)].rearrange("o c n -> (o c) n")).then_inc(s["x_loaded"], 16)
                    take(sp, "adjT_free")
                    sp.dma_start(adjT_sb, adjT[bass.ds(b, 1)].rearrange("o (t p) n -> p (o t) n", p=P)).then_inc(
                        s["adjT_loaded"], 16)
                    take(sp, "adj_loaded", 16)
                    sp.sem_inc(s["adj_for_dve"], 1)
                    sp.sem_inc(s["adj_for_act"], 1)
                    for t in range(T):
                        q = t % 2
                        take(sp, f"key_ready{q}")
                        sp.dma_start(key_rows[bass.ds(b * N + t * P, P), 0:N], key_out[:, q, :]).then_inc(
                            s[f"key_stored{q}"], 16)
                        if t == 3:
                            take(sp, "x1_ready")
                            dst = x1_rows[bass.ds(b * N, N)].rearrange("(t p) c -> p t c", p=P)
                            sp.dma_start(dst, x1_sb[:]).then_inc(s["x1_stored"], 16)
                            

            @block.scalar
            def _(act):
                a = nc.scalar
                act.sem_inc(s["adj_free"], 1)
                with act.Fori(0, B) as b:
                    take(act, "adj_for_act")
                    for t in range(T):
                        last = a.activation(act_junk[:], adj_sb[:, t, :], ACT.Copy, accum_out=deg[:, t:t + 1])
                        last.then_inc(astep, 1)
                        act.wait_ge(astep, t + 1)
                    act.sem_inc(s["adj_free"], 1)
                    act.sem_inc(s["deg_ready"], 1)
                    act.sem_clear(astep)
                    for h in range(2):
                        take(act, "half_projected")
                        a.copy(proj[:, bass.ts(h, T // 2), :], proj_ps[:]).then_inc(astep, 1)
                        act.wait_ge(astep, h + 1)
                        act.sem_inc(s["half_copied"], 1)
                    act.sem_inc(s["proj_ready"], 1)
                    act.sem_clear(astep)
                    for t in range(T):
                        q = t % 2
                        take(act, f"key_for_act{q}")
                        a.activation(act_junk[:], key_out[:, q, :], ACT.Sign,
                                     accum_out=m_batch[:, t:t + 1]).then_inc(astep, 1)
                        act.wait_ge(astep, t + 1)
                        act.sem_inc(s[f"key_counted{q}"], 1)
                    act.sem_clear(astep)
                    a.copy(m_all[:, bass.ds(b * T, T)], m_batch[:]).then_inc(astep, 1)
                    act.wait_ge(astep, 1)
                    act.sem_clear(astep)

            @block.gpsimd
            def _(pool):
                with pool.Fori(0, B) as b:
                    take(pool, "safe_ready")
                    nc.gpsimd.tensor_tensor(dpow[:], safe_deg[:], power[:], ALU.pow).then_inc(s["pow_ready"], 1)
                    take(pool, "var_ready")
                    nc.gpsimd.tensor_tensor(rstd[:], var[:], power[:], ALU.pow).then_inc(s["rstd_ready"], 1)

            @block.tensor
            def _(pe):
                pe.sem_inc(s["adjT_free"], 1)
                pe.sem_inc(s["x_free"], 1)
                with pe.Fori(0, B) as b:
                    take(pe, "x_loaded", 32)
                    for h in range(2):
                        for u in range(T // 2):
                            mm = nc.tensor.matmul(proj_ps[:, u, :], xT_sb[:, bass.ts(h * T // 2 + u, P)], wcat_sb[:],
                                                  start=True, stop=True)
                        mm.then_inc(s["half_projected"], 1)
                        take(pe, "half_copied")
                    pe.sem_inc(s["x_free"], 1)
                    take(pe, "adjT_loaded", 16)
                    for r in range(K0 - 1):
                        take(pe, "z_ready")
                        for t in range(T):
                            for j in range(T):
                                mm = nc.tensor.matmul(y_ps[:, t, :], adjT_sb[:, j, bass.ts(t, P)], z[:, j, :],
                                                      start=(j == 0), stop=(j == T - 1))
                        mm.then_inc(s["y_ready"], 1)
                    mm = nc.tensor.matmul(proj_ps[:, 0, 0:C], ident[:], ones[:, 0:C], start=True, stop=True)
                    mm.then_inc(astep_pe, 1)
                    pe.wait_ge(astep_pe, 1)
                    pe.sem_clear(astep_pe)
                    pe.sem_inc(s["adjT_free"], 1)
                    take(pe, "removed_ready")
                    for t in range(T):
                        q = t % 2
                        take(pe, f"rem_free{q}")
                        for g in range(2):
                            half = rem_ps[q][:, bass.ts(g, 512)]
                            nc.tensor.matmul(half, ident_b[:], removed[:, t, bass.ts(g, 512)], start=True, stop=False)
                            for j in range(4):
                                mm = nc.tensor.matmul(half[:, bass.ts(j, P)], removed[:, g * 4 + j, bass.ts(t, P)],
                                                      ident_b[:], start=False, stop=(j == 3))
                        mm.then_inc(s[f"rem_ready{q}"], 1)

            @block.vector
            def _(dve):
                v = nc.vector
                count = [0]

                def done(*instructions):
                    for i in instructions:
                        i.then_inc(step, 1)
                    count[0] += len(instructions)
                    dve.wait_ge(step, count[0])

                def wide(ap):
                    return ap.unsqueeze(2).to_broadcast([P, T, C])

                def apply_laplacian(src, add_to, factor, minus, dst):
                    take(dve, "y_ready")
                    done(v.tensor_tensor(tmp[:], y_ps[:], wide(dsc[:]), ALU.mult),
                         v.tensor_tensor(tmp2[:], src, wide(keep[:]), ALU.mult))
                    done(v.tensor_tensor(tmp[:], tmp2[:], tmp[:], ALU.subtract))
                    done(v.scalar_tensor_tensor(out=dst, in0=tmp[:], scalar=factor, in1=add_to, op0=ALU.mult,
                                                op1=ALU.add))
                    if minus is not None:
                        done(v.tensor_tensor(dst, dst, minus, ALU.subtract))

                def start_product(src):
                    done(v.tensor_tensor(z[:], src, wide(dsc[:]), ALU.mult))
                    dve.sem_inc(s["z_ready"], 1)

                def order(k):
                    return proj[:, :, k * C:(k + 1) * C]

                dve.sem_inc(s["adj_free"], 1)
                dve.sem_inc(s["x_free"], 1)
                for q in range(2):
                    dve.sem_inc(s[f"rem_free{q}"], 1)
                    dve.sem_inc(s[f"key_counted{q}"], 1)
                    dve.sem_inc(s[f"key_stored{q}"], 16)
                dve.sem_inc(s["x1_stored"], 16)
                with dve.Fori(0, B) as b:
                    count[0] = 0
                    take(dve, "adj_for_dve")
                    for t in range(T):
                        done(v.scalar_tensor_tensor(out=nbkey[:, t, :], in0=adj_sb[:, t, :], scalar=0.0, in1=down[:],
                                                    op0=ALU.is_gt, op1=ALU.mult))
                        done(v.tensor_tensor(nbkey[:, t, bass.ts(t, P)], nbkey[:, t, bass.ts(t, P)], off_diag[:],
                                             ALU.mult))
                        done(v.tensor_scalar(nb[:], nbkey[:, t, :], 1.0, None, ALU.min))
                        done(v.tensor_tensor_scan(rank[:], ones_row[:], nb[:], 0.0, ALU.mult, ALU.add))
                        done(v.tensor_tensor(ranked[:, t, :], rank[:], nb[:], ALU.mult),
                             v.tensor_copy(nb_count[:, t:t + 1], rank[:, N - 1:N]))
                        if t == 1:
                            take(dve, "deg_ready")
                            done(v.tensor_scalar(safe_deg[:], deg[:], 1e-37, None, ALU.max),
                                 v.tensor_scalar(keep[:], deg[:], 0.0, None, ALU.not_equal),
                                 v.tensor_scalar(dsc[:], deg[:], 0.0, None, ALU.is_gt))
                            dve.sem_inc(s["safe_ready"], 1)
                        if t == 2:
                            take(dve, "pow_ready")
                            done(v.tensor_tensor(dsc[:], dsc[:], dpow[:], ALU.mult))
                            take(dve, "proj_ready")
                            start_product(order(3))
                        if t == 4:
                            apply_laplacian(order(3), order(2), 2.0, None, bb[0][:])
                            start_product(bb[0][:])
                        if t == 6:
                            apply_laplacian(bb[0][:], order(1), 2.0, order(3), bb[1][:])
                            start_product(bb[1][:])
                    dve.sem_inc(s["adj_free"], 1)
                    done(v.tensor_copy(count_i[:], nb_count[:]), v.tensor_copy(mask_b[:], mask_f[:, bass.ds(b * T, T)]),
                         v.tensor_scalar(dil[:], nb_count[:], float(T_THRESH), None, ALU.is_gt))
                    done(v.tensor_scalar(odd_i[:], count_i[:], 1, None, ALU.bitwise_and),
                         v.tensor_tensor(dil[:], dil[:], mask_b[:], ALU.mult))
                    done(v.tensor_copy(even[:], odd_i[:]), v.tensor_tensor(half_i[:], count_i[:], odd_i[:], ALU.add))
                    done(v.tensor_scalar(half_i[:], half_i[:], 1, None, ALU.logical_shift_right),
                         v.tensor_scalar(even[:], even[:], -1.0, 1.0, ALU.mult, ALU.add))
                    done(v.tensor_scalar(hit1[:], half_i[:], 1.0, None, ALU.add),
                         v.scalar_tensor_tensor(out=hit2[:], in0=nb_count[:], scalar=1.0, in1=even[:], op0=ALU.add,
                                                op1=ALU.mult))
                    done(v.tensor_tensor(hit1[:], hit1[:], dil[:], ALU.mult),
                         v.tensor_tensor(hit2[:], hit2[:], dil[:], ALU.mult))
                    done(v.tensor_scalar(hit1[:], hit1[:], -1.0, None, ALU.add),
                         v.tensor_scalar(hit2[:], hit2[:], -1.0, None, ALU.add))
                    for t in range(T):
                        done(v.tensor_scalar(first_hit[:], ranked[:, t, :], hit1[:, t:t + 1], None, ALU.is_equal))
                        done(v.scalar_tensor_tensor(out=removed[:, t, :], in0=ranked[:, t, :], scalar=hit2[:, t:t + 1],
                                                    in1=first_hit[:], op0=ALU.is_equal, op1=ALU.add))
                    dve.sem_inc(s["removed_ready"], 1)
                    done(v.tensor_tensor(tmp2[:], order(0), bb[0][:], ALU.subtract))
                    done(v.tensor_tensor(bb[2][:], tmp2[:], x_sb[:], ALU.add))
                    done(v.tensor_tensor(bb[2][:], bb[2][:], bias0_sb[:].unsqueeze(1).to_broadcast([P, T, C]),
                                         ALU.add))
                    dve.sem_inc(s["x_free"], 1)
                    apply_laplacian(bb[1][:], bb[2][:], 1.0, None, bb[0][:])
                    done(v.tensor_reduce(mean[:], bb[0][:], AX_X, ALU.add))
                    done(v.tensor_scalar(mean[:], mean[:], 1.0 / C, None, ALU.mult))
                    done(v.tensor_tensor(bb[1][:], bb[0][:], wide(mean[:]), ALU.subtract))
                    done(v.tensor_tensor(tmp[:], bb[1][:], bb[1][:], ALU.mult))
                    done(v.tensor_reduce(var[:], tmp[:], AX_X, ALU.add))
                    done(v.tensor_scalar(var[:], var[:], 1.0 / C, EPS, ALU.mult, ALU.add))
                    dve.sem_inc(s["var_ready"], 1)
                    for t in range(T):
                        q = t % 2
                        take(dve, f"rem_ready{q}")
                        take(dve, f"key_stored{q}", 16)
                        take(dve, f"key_counted{q}")
                        done(v.scalar_tensor_tensor(out=key_out[:, q, :], in0=rem_ps[q][:], scalar=0.0,
                                                    in1=nbkey[:, t, :], op0=ALU.is_equal, op1=ALU.mult))
                        dve.sem_inc(s[f"rem_free{q}"], 1)
                        done(v.tensor_tensor(key_out[:, q, bass.ts(t, P)], key_out[:, q, bass.ts(t, P)],
                                             diag_key[:, bass.ts(t, P)], ALU.add))
                        dve.sem_inc(s[f"key_ready{q}"], 1)
                        dve.sem_inc(s[f"key_for_act{q}"], 1)
                        if t == 1:
                            take(dve, "rstd_ready")
                            take(dve, "x1_stored", 16)
                            done(v.tensor_tensor(x1_sb[:], bb[1][:], wide(rstd[:]), ALU.mult))
                            dve.sem_inc(s["x1_ready"], 1)
                    dve.sem_clear(step)
                for q in range(2):
                    take(dve, f"key_stored{q}", 16)
                take(dve, "x1_stored", 16)

        ids_all = sb("ids_all", [P, TILES], I32)

        with ExitStack() as bctx:
            def bsb(name, shape, dt):
                return bctx.enter_context(nc.sbuf_tensor(name, shape, dt))

            def bsem(name):
                return bctx.enter_context(nc.semaphore(name))

            NL = len(LEVELS)
            meta = bsb("meta", [P, COLS, META], F32)
            q_f = bsb("q_f", [P, COLS], F32)
            q_i = bsb("q_i", [P, COLS], I32)
            r_i = bsb("r_i", [P, COLS], I32)
            frac = bsb("frac", [P, COLS], F32)
            at_level = bsb("at_level", [P, NL, COLS], F32)
            above = bsb("above", [P, COLS], F32)
            ahead = bsb("ahead", [P, COLS], F32)
            colsum = bsb("colsum", [P, COLS], F32)
            place = bsb("place", [P, COLS], F32)
            place_i = bsb("place_i", [P, COLS], I32)
            table_at = bsb("table_at", [P, COLS], I32)
            first_tile = bsb("first_tile", [P, NL + 1], F32)
            total = bsb("total", [P, NL], F32)
            total_i = bsb("total_i", [P, NL], I32)
            node_i = bsb("node_i", [P, COLS], I32)
            node_p = bsb("node_p", [P, COLS], I32)
            pads = bsb("pads", [P, lists.shape[0] // P], I32)
            count_ps = bctx.enter_context(nc.psum_tensor("count_ps", [P, 2, 1024], F32))
            records_ready, nodes_ready, counted, level_ready, places_ready, pads_ready, pads_stored, stored, listed, listed_all = (
                bsem(n) for n in ("records_ready", "nodes_ready", "counted", "level_ready", "places_ready",
                                  "pads_ready", "pads_stored", "records_stored", "listed", "listed_all"))
            block = bctx.enter_context(nc.Block())

            @block.sync
            def _(sp):
                sp.wait_ge(pads_ready, 1)
                sp.dma_start(lists.rearrange("(p k) o -> p (k o)", p=P), pads[:]).then_inc(pads_stored, 16)
                sp.wait_ge(records_ready, 1)
                sp.dma_start(key_rows[0:NODES, N:ROW].rearrange("(c p) k -> p c k", p=P),
                             meta[:].rearrange("p c k -> p (c k)").bitcast(F16).rearrange(
                                 "p (c k) -> p c k", c=COLS)).then_inc(stored, 16)
                sp.wait_ge(listed_all, 1)
                sp.dma_start(ids_all[:], lists[0:TABLE].rearrange("(p t) o -> p (t o)", p=P)).then_inc(stored, 16)
                sp.wait_ge(stored, 32)

            @block.gpsimd
            def _(pool):
                nc.gpsimd.iota(node_i[:], pattern=[[P, COLS]], base=0, channel_multiplier=1).then_inc(nodes_ready, 1)
                pool.wait_ge(nodes_ready, 1)
                pool.wait_ge(pads_stored, 16)
                pool.wait_ge(places_ready, 1)
                for c in range(COLS):
                    pool.indirect_dma_start(lists, bass.IndirectOffsetOnAxis(ap=place_i[:, c:c + 1].bitcast(U32), axis=0),
                                            node_i[:, c:c + 1], None).then_inc(listed, 16)
                pool.wait_ge(listed, 16 * COLS)
                pool.sem_inc(listed_all, 1)

            @block.tensor
            def _(pe):
                pe.wait_ge(level_ready, 1)
                flat = at_level[:].rearrange("p l c -> p (l c)")
                for g in range(2):
                    lhs = (before, ones)[g]
                    for first in range(0, NL * COLS, 512):
                        n = min(512, NL * COLS - first)
                        mm = nc.tensor.matmul(count_ps[:, g, first:first + n], lhs[:], flat[:, first:first + n],
                                              start=True, stop=True)
                mm.then_inc(counted, 1)

            @block.vector
            def _(dve):
                v = nc.vector
                count = [0]

                def done(*instructions):
                    for i in instructions:
                        i.then_inc(step, 1)
                    count[0] += len(instructions)
                    dve.wait_ge(step, count[0])

                done(v.memset(pads[:], NODES), v.memset(meta[:], 0.0), v.memset(first_tile[:], 0.0))
                dve.sem_inc(pads_ready, 1)
                for i, (tau, wt) in enumerate(zip(TAUS, QWEIGHTS)):
                    done(v.tensor_scalar(q_f[:], m_all[:], -1.0, tau * 4, ALU.add, ALU.mult))
                    done(v.tensor_copy(q_i[:], q_f[:]))
                    done(v.tensor_scalar(r_i[:], q_i[:], 3, None, ALU.bitwise_and))
                    done(v.tensor_scalar(q_i[:], q_i[:], 2, None, ALU.logical_shift_right))
                    done(v.tensor_copy(meta[:, :, i], q_i[:]), v.tensor_scalar(frac[:], r_i[:], 0.25, None, ALU.mult))
                    done(v.tensor_scalar(meta[:, :, W_LOW + i], frac[:], -wt, wt, ALU.mult, ALU.add),
                         v.tensor_scalar(meta[:, :, W_UP + i], frac[:], wt, None, ALU.mult))
                dve.wait_ge(nodes_ready, 1)
                shift = N.bit_length() - 1
                done(v.tensor_scalar(node_p[:], node_i[:], shift, shift, ALU.logical_shift_right,
                                     ALU.logical_shift_left))
                done(v.tensor_scalar(meta[:, :, FIRST], node_p[:], float(N), None, ALU.add),
                     v.tensor_scalar(meta[:, :, TO_PAD], node_p[:], -1.0, float(NODES - N), ALU.mult, ALU.add),
                     v.tensor_copy(meta[:, :, NODE], node_i[:]))
                dve.sem_inc(records_ready, 1)
                low = 0
                for i, cap in enumerate(LEVELS):
                    done(v.tensor_scalar(above[:], m_all[:], float(low), None, ALU.is_gt))
                    done(v.scalar_tensor_tensor(out=at_level[:, i, :], in0=m_all[:], scalar=float(cap), in1=above[:],
                                                op0=ALU.is_le, op1=ALU.mult))
                    low = cap
                dve.sem_inc(level_ready, 1)
                dve.wait_ge(counted, 1)
                for i, cap in enumerate(LEVELS):
                    done(v.tensor_copy(colsum[:], count_ps[:, 1, bass.ts(i, COLS)]))
                    done(v.tensor_tensor_scan(ahead[:], ones[:, 0:COLS], colsum[:], 0.0, ALU.mult, ALU.add))
                    done(v.tensor_copy(total[:, i:i + 1], ahead[:, COLS - 1:COLS]),
                         v.tensor_tensor(colsum[:], ahead[:], colsum[:], ALU.subtract))
                    done(v.tensor_tensor(colsum[:], colsum[:], count_ps[:, 0, bass.ts(i, COLS)], ALU.add))
                    lanes = P if cap in WIDE else P // NARROW[cap]
                    size_bits = lanes.bit_length() - 1
                    done(v.tensor_scalar(total[:, i:i + 1], total[:, i:i + 1], float(lanes - 1), None, ALU.add),
                         v.tensor_copy(place_i[:], colsum[:]))
                    done(v.tensor_copy(total_i[:, i:i + 1], total[:, i:i + 1]))
                    done(v.tensor_scalar(total_i[:, i:i + 1], total_i[:, i:i + 1], size_bits, None,
                                         ALU.logical_shift_right))
                    if cap in WIDE:
                        done(v.tensor_scalar(total[:, i:i + 1], total_i[:, i:i + 1], 1.0, None, ALU.max),
                             v.tensor_scalar(table_at[:], place_i[:], P - 1, None, ALU.bitwise_and),
                             v.tensor_scalar(place_i[:], place_i[:], size_bits, None, ALU.logical_shift_right))
                        done(v.tensor_copy(tiles_of[:, i:i + 1], total[:, i:i + 1]),
                             v.tensor_tensor(first_tile[:, i + 1:i + 2], first_tile[:, i:i + 1], total[:, i:i + 1],
                                             ALU.add),
                             v.scalar_tensor_tensor(out=colsum[:], in0=table_at[:], scalar=float(TILES),
                                                    in1=place_i[:], op0=ALU.mult, op1=ALU.add))
                        done(v.scalar_tensor_tensor(out=colsum[:], in0=colsum[:], scalar=first_tile[:, i:i + 1],
                                                    in1=at_level[:, i, :], op0=ALU.add, op1=ALU.mult))
                    else:
                        done(v.tensor_copy(tiles_of[:, i:i + 1], total_i[:, i:i + 1]),
                             v.scalar_tensor_tensor(out=colsum[:], in0=colsum[:],
                                                    scalar=float(TABLE + (i - len(WIDE)) * LIST),
                                                    in1=at_level[:, i, :], op0=ALU.add, op1=ALU.mult))
                    if i == 0:
                        done(v.tensor_copy(place[:], colsum[:]))
                    else:
                        done(v.tensor_tensor(place[:], place[:], colsum[:], ALU.add))
                done(v.tensor_copy(place_i[:], place[:]),
                     v.tensor_copy(tiles_of[:, NL:NL + 1], first_tile[:, len(WIDE):len(WIDE) + 1]))
                dve.sem_inc(places_ready, 1)
                dve.sem_clear(step)

        def emit_find(v, done, keys, found, rounds):
            for r in range(rounds):
                done(v.max(found[:, bass.ts(r, 8)], keys))
                if r + 1 < rounds:
                    done(v.match_replace(keys, found[:, bass.ts(r, 8)], keys, 0.0))

        def emit_stage(v, src, dst, cap, width, p, k):
            compared, kept = stage_parts(cap, p, k)
            ops = []

            def view(buf, first, step_, blocks, n):
                if blocks == 1:
                    return buf[:, first * width:(first + n) * width].rearrange("q (b w) -> q b w", b=1)
                whole = buf[:, 0:blocks * step_ * width].rearrange("q (b w) -> q b w", b=blocks)
                return whole[:, :, first * width:(first + n) * width]

            for first, step_, blocks, groups, n in compared:
                if groups > 1 or n == k:
                    span = groups * 2 * k
                    a, z = (view(x_, first, step_, blocks, span).rearrange("q b (g two w) -> q b g two w", two=2,
                                                                         w=k * width) for x_ in (src, dst))
                    a0, a1, z0, z1 = a[:, :, :, 0, :], a[:, :, :, 1, :], z[:, :, :, 0, :], z[:, :, :, 1, :]
                else:
                    a0, a1, z0, z1 = (view(x_, first + d, step_, blocks, n) for x_ in (src, dst) for d in (0, k))
                ops += [v.tensor_tensor(z0, a0, a1, ALU.min), v.tensor_tensor(z1, a0, a1, ALU.max)]
            for first, step_, blocks, n in kept:
                ops.append(v.tensor_copy(view(dst, first, step_, blocks, n), view(src, first, step_, blocks, n)))
            return ops

        def emit_aggregate(v, done, at, other, record, weights, weight, agg, cap, width):
            for first in range(0, cap, 256):
                n = min(256, cap - first)
                done(*[v.tensor_scalar(weights[:, q + 3 * ahead_by, 0:n], ramp[:, first:first + n],
                                       record[:, LOWER + q:LOWER + q + 1], record[:, col + q:col + q + 1],
                                       ALU.is_equal, ALU.mult)
                       for q in range(len(TAUS)) for ahead_by, ramp, col in ((0, up, W_LOW), (1, up_less, W_UP))])
                done(v.tensor_reduce(weight[:, first:first + n], weights[:, :, 0:n].rearrange("p q k -> p k q"), AX_X,
                                     ALU.add))
            done(v.tensor_tensor(other[:, 0:cap * width].rearrange("p (k c) -> p k c", c=width),
                                 at[:, 0:cap * width].rearrange("p (k c) -> p k c", c=width),
                                 weight[:, 0:cap].unsqueeze(2).to_broadcast([P, cap, width]), ALU.mult))
            done(v.tensor_reduce(agg, other[:, 0:cap * width].rearrange("p (k c) -> p c k", c=width), AX_X, ALU.add))

        def get(eng, semaphore, n=1):
            eng.wait_ge(semaphore, n)
            eng.sem_clear(semaphore)

        cctx = ctx.enter_context(ExitStack())

        def csb(name, shape, dt):
            return cctx.enter_context(nc.sbuf_tensor(name, shape, dt))

        found = csb("found", [P, max(WIDE)], F32)
        unused = csb("unused", [P, max(WIDE)], F32)
        nbr_f = csb("nbr_f", [P, max(WIDE)], F32)
        nbr_next = csb("nbr_next", [P, max(WIDE)], I32)
        nbr = csb("nbr", [P, max(WIDE)], I32)
        weights = csb("weights", [P, 2 * len(TAUS), 256], F32)
        weight = csb("weight", [P, N], F32)
        ids = csb("ids", [P, 1], I32)
        keys_in = csb("keys_in", [P, ROW], F16)
        keys = csb("keys", [P, ROW], F16)
        record = csb("record", [P, META], F32)
        record_next = csb("record_next", [P, META], F32)
        agg = csb("agg", [P, C], F32)
        agg_out = csb("agg_out", [P, C], F32)
        to_row = csb("to_row", [P, 1], I32)
        out_ids = csb("out_ids", [P, 1], I32)
        gathering = csb("gathering", [P, max(WIDE) * C], F32)

        with ExitStack() as wctx:
            keys_wanted, keys_landed, keys_free, keys_ready, go, gathered, dma_done = (
                wctx.enter_context(nc.semaphore(n)) for n in (
                    "keys_wanted", "keys_landed", "keys_free", "keys_ready", "go", "gathered", "gather_dmas"))
            astep = wctx.enter_context(nc.semaphore("astep_c"))
            block = wctx.enter_context(nc.Block())

            @block.scalar
            def _(act):
                n = act.value_load(tiles_of[0:1, len(LEVELS):len(LEVELS) + 1], min_val=len(WIDE), max_val=TILES)
                nc.scalar.copy(ids[:], ids_all[:, 0:1]).then_inc(astep, 1)
                get(act, astep)
                act.sem_inc(keys_wanted, 1)
                with act.Fori(0, TILES - 1) as t:
                    with act.If(t < n + 1):
                        get(act, keys_landed)
                        get(act, keys_free)
                        nc.scalar.copy(keys[:], keys_in[:]).then_inc(astep, 1)
                        nc.scalar.copy(ids[:], ids_all[:, bass.ds(t + 1, 1)]).then_inc(astep, 1)
                        get(act, astep, 2)
                        act.sem_inc(keys_ready, 1)
                        act.sem_inc(keys_wanted, 1)
                    with act.Else():
                        act.nop()
                    act.nop()

            @block.gpsimd
            def _(pool):
                def load_keys():
                    get(pool, keys_wanted)
                    pool.indirect_dma_start(keys_in[:], None, key_rows,
                                            bass.IndirectOffsetOnAxis(ap=ids[:].bitcast(U32), axis=0)).then_inc(
                        dma_done, 16)

                def store_agg():
                    pool.indirect_dma_start(agg_rows, bass.IndirectOffsetOnAxis(ap=out_ids[:].bitcast(U32), axis=0),
                                            agg_out[:], None, bounds_check=NODES - 1, oob_is_err=False).then_inc(
                        dma_done, 16)

                for _ in range(2):
                    load_keys()
                    pool.drain().then_inc(keys_landed, 1)
                for level, cap in enumerate(WIDE):
                    n = pool.value_load(tiles_of[0:1, level:level + 1], min_val=1, max_val=NODES // P)
                    with pool.Fori(0, NODES // P) as i:
                        with pool.If(i < n):
                            get(pool, go)
                            for k in range(cap):
                                pool.indirect_dma_start(gathering[:, k * C:(k + 1) * C], None, x1_rows,
                                                        bass.IndirectOffsetOnAxis(ap=nbr[:, k:k + 1].bitcast(U32),
                                                                                  axis=0)).then_inc(dma_done, 16)
                            store_agg()
                            load_keys()
                            pool.drain().then_inc(gathered, 1)
                            pool.sem_inc(keys_landed, 1)
                        with pool.Else():
                            pool.nop()
                        pool.nop()
                for _ in range(2):
                    get(pool, go)
                    store_agg()
                    pool.drain().then_inc(gathered, 1)

            @block.vector
            def _(dve):
                v = nc.vector
                count = [0]

                def done(*instructions):
                    for i in instructions:
                        i.then_inc(step, 1)
                    count[0] += len(instructions)
                    dve.wait_ge(step, count[0])

                def restart():
                    dve.sem_clear(step)
                    count[0] = 0

                def find_neighbours(cap):
                    get(dve, keys_ready)
                    emit_find(v, done, keys[:, 0:N], found, -(-cap // 8))
                    meta_in = keys[:, N:ROW].bitcast(F32)
                    f = found[:, 0:cap]
                    done(v.tensor_scalar(unused[:, 0:cap], f, 0.0, meta_in[:, TO_PAD:TO_PAD + 1], ALU.is_equal,
                                         ALU.mult),
                         v.tensor_scalar(nbr_f[:, 0:cap], f, -1.0, meta_in[:, FIRST:FIRST + 1], ALU.mult, ALU.add),
                         v.tensor_copy(record_next[:], meta_in))
                    dve.sem_inc(keys_free, 1)
                    done(v.tensor_tensor(nbr_next[:, 0:cap], nbr_f[:, 0:cap], unused[:, 0:cap], ALU.add))

                def hand_over(first):
                    return [v.tensor_copy(nbr[:], nbr_next[:]), v.tensor_copy(agg_out[:], agg[:]),
                            v.tensor_copy(out_ids[:], to_row[:])]

                def tile(cap, next_cap):
                    done(v.tensor_copy(record[:], record_next[:]))
                    if next_cap:
                        find_neighbours(next_cap)
                    get(dve, gathered)
                    stages = list(sort_stages(cap))
                    done(*emit_stage(v, gathering, slots[0], cap, C, *stages[0]), *hand_over(False))
                    dve.sem_inc(go, 1)
                    src, dst = slots[0], slots[1]
                    for p, k in stages[1:]:
                        done(*emit_stage(v, src, dst, cap, C, p, k))
                        src, dst = dst, src
                    emit_aggregate(v, done, src, dst, record, weights, weight, agg[:], cap, C)
                    done(v.tensor_copy(to_row[:], record[:, NODE:NODE + 1]))
                    restart()

                done(v.memset(to_row[:], NODES), v.memset(agg[:], 0.0), v.memset(nbr_next[:], 0))
                dve.sem_inc(keys_free, 1)
                find_neighbours(WIDE[0])
                done(*hand_over(True))
                dve.sem_inc(go, 1)
                restart()
                for level, cap in enumerate(WIDE):
                    n = dve.value_load(tiles_of[0:1, level:level + 1], min_val=1, max_val=NODES // P)
                    with dve.Fori(0, NODES // P) as i:
                        with dve.If(i + 1 < n):
                            tile(cap, cap)
                        with dve.Else():
                            dve.nop()
                        dve.nop()
                    tile(cap, WIDE[level + 1] if level + 1 < len(WIDE) else 0)
                get(dve, gathered)
                done(*hand_over(False))
                dve.sem_inc(go, 1)
                get(dve, gathered)
                restart()

        with ExitStack() as nctx:
            stage = nctx.enter_context(nc.sbuf_tensor("stage", [P, BLOCK, C // min(NARROW.values())], F32))
            ids_free, ids_loaded, tile_loaded, tile_ready, nbr_ready, dma_done, gathered, agg_ready = (
                nctx.enter_context(nc.semaphore(n)) for n in (
                    "ids_free", "ids_loaded", "tile_loaded", "tile_ready", "nbr_ready", "narrow_dmas",
                    "narrow_gathered", "agg_ready"))
            block = nctx.enter_context(nc.Block())

            def each_tile(eng, level, body):
                most = NODES * NARROW[LEVELS[level]] // P
                n = eng.value_load(tiles_of[0:1, level:level + 1], min_val=0, max_val=most)
                inner = 16
                with eng.Fori(0, most // inner) as o:
                    with eng.If(o * inner < n):
                        with eng.Fori(0, inner) as i:
                            with eng.If(o * inner + i < n):
                                body(o * inner + i)
                            with eng.Else():
                                eng.nop()
                            eng.nop()
                        eng.nop()
                    with eng.Else():
                        eng.nop()
                    eng.nop()

            @block.sync
            def _(sp):
                for level in range(len(WIDE), len(LEVELS)):
                    groups = NARROW[LEVELS[level]]
                    lanes = P // groups
                    start = TABLE + (level - len(WIDE)) * LIST

                    def load_ids(i, groups=groups, lanes=lanes, start=start):
                        get(sp, ids_free)
                        for g in range(groups):
                            sp.dma_start(ids[bass.ts(g, lanes), :],
                                         lists[bass.ds(i * lanes + start, lanes)]).then_inc(ids_loaded, 16)
                        get(sp, ids_loaded, 16 * groups)
                        sp.sem_inc(tile_loaded, 1)
                    each_tile(sp, level, load_ids)

            @block.gpsimd
            def _(pool):
                pool.sem_inc(ids_free, 1)
                for level in range(len(WIDE), len(LEVELS)):
                    cap = LEVELS[level]
                    groups = NARROW[cap]
                    width = C // groups

                    def tile(i, cap=cap, groups=groups, width=width):
                        get(pool, tile_loaded)
                        pool.indirect_dma_start(keys_in[:], None, key_rows,
                                                bass.IndirectOffsetOnAxis(ap=ids[:].bitcast(U32), axis=0)).then_inc(
                            dma_done, 16)
                        pool.drain().then_inc(tile_ready, 1)
                        with pool.Fori(0, cap // BLOCK):
                            get(pool, nbr_ready)
                            for k in range(BLOCK):
                                pool.indirect_dma_start(stage[:].rearrange("p k c -> p (k c)")[:, bass.ts(k, width)], None,
                                                        x1_rows.rearrange("n (g c) -> (n g) c", g=groups),
                                                        bass.IndirectOffsetOnAxis(ap=nbr[:, k:k + 1].bitcast(U32),
                                                                                  axis=0)).then_inc(dma_done, 16)
                            pool.drain().then_inc(gathered, 1)
                        get(pool, agg_ready)
                        pool.indirect_dma_start(agg_rows.rearrange("n (g c) -> (n g) c", g=groups),
                                                bass.IndirectOffsetOnAxis(ap=out_ids[:].bitcast(U32), axis=0),
                                                agg[:, 0:width], None, bounds_check=NODES * groups - 1,
                                                oob_is_err=False).then_inc(dma_done, 16)
                        pool.drain().then_inc(ids_free, 1)
                    each_tile(pool, level, tile)

            @block.vector
            def _(dve):
                v = nc.vector
                count = [0]

                def done(*instructions):
                    for i in instructions:
                        i.then_inc(step, 1)
                    count[0] += len(instructions)
                    dve.wait_ge(step, count[0])

                def restart():
                    dve.sem_clear(step)
                    count[0] = 0

                for level in range(len(WIDE), len(LEVELS)):
                    cap = LEVELS[level]
                    groups = NARROW[cap]
                    width = C // groups

                    def tile(i, cap=cap, groups=groups, width=width):
                        get(dve, tile_ready)
                        record_in = keys_in[:, N:ROW].bitcast(F32)
                        done(v.tensor_copy(record[:], record_in),
                             v.tensor_scalar(out_ids[:], ids[:], float(groups), group_f[groups][:, 0:1], ALU.mult,
                                             ALU.add))
                        restart()
                        with dve.Fori(0, cap // BLOCK) as blk:
                            f = found[:, 0:BLOCK]
                            emit_find(v, done, keys_in[:, 0:N], found, BLOCK // 8)
                            done(v.match_replace(keys_in[:, 0:N], found[:, BLOCK - 8:BLOCK], keys_in[:, 0:N], 0.0),
                                 v.tensor_scalar(unused[:, 0:BLOCK], f, 0.0, record[:, TO_PAD:TO_PAD + 1],
                                                 ALU.is_equal, ALU.mult),
                                 v.tensor_scalar(nbr_f[:, 0:BLOCK], f, -1.0, record[:, FIRST:FIRST + 1], ALU.mult,
                                                 ALU.add))
                            done(v.tensor_tensor(nbr_f[:, 0:BLOCK], nbr_f[:, 0:BLOCK], unused[:, 0:BLOCK], ALU.add))
                            done(v.tensor_scalar(nbr[:, 0:BLOCK], nbr_f[:, 0:BLOCK], float(groups),
                                                 group_f[groups][:, 0:1], ALU.mult, ALU.add))
                            dve.sem_inc(nbr_ready, 1)
                            get(dve, gathered)
                            done(v.tensor_copy(slots[0][:, bass.ds(blk * (BLOCK * width), BLOCK * width)],
                                               stage[:].rearrange("p k c -> p (k c)")[:, 0:BLOCK * width]))
                            restart()
                        src, dst = slots[0], slots[1]
                        for p, k in sort_stages(cap):
                            done(*emit_stage(v, src, dst, cap, width, p, k))
                            src, dst = dst, src
                        emit_aggregate(v, done, src, dst, record, weights, weight, agg[:, 0:width], cap, width)
                        dve.sem_inc(agg_ready, 1)
                        restart()
                    each_tile(dve, level, tile)

        with ExitStack() as dctx:
            def dsb(name, shape, dt):
                return dctx.enter_context(nc.sbuf_tensor(name, shape, dt))

            def dsem(name):
                return dctx.enter_context(nc.semaphore(name))

            x1_in = [dsb(f"x1_in{i}", [P, T, C], F32) for i in range(2)]
            agg_in = [dsb(f"agg_in{i}", [P, T, C], F32) for i in range(2)]
            res = dsb("res", [P, T, C], F32)
            resT = dsb("resT", [C, N], F32)
            hidT = dsb("hidT", [H, N], F32)
            y = dsb("y", [P, T, C], F32)
            cen = dsb("cen", [P, T, C], F32)
            sq = dsb("sq", [P, T, C], F32)
            mean = dsb("mean_d", [P, T], F32)
            var = dsb("var_d", [P, T], F32)
            rstd = dsb("rstd_d", [P, T], F32)
            fin = [dsb(f"fin{i}", [P, T, C], F32) for i in range(2)]
            resT_ps = dctx.enter_context(nc.psum_tensor("resT_ps", [C, N], F32))
            hid_ps = dctx.enter_context(nc.psum_tensor("hid_ps", [H, N], F32))
            out_ps = dctx.enter_context(nc.psum_tensor("out_ps", [P, T, C], F32))
            in_loaded = [dsem(f"in_loaded{i}") for i in range(2)]
            fin_stored = [dsem(f"fin_stored{i}") for i in range(2)]
            in_used, res_ready, resT_ready, resT_copied, hid_ready, hid_act, out_ready, y_done, var_ready, rstd_ready, fin_ready = (
                dsem(n) for n in ("in_used", "res_ready", "resT_ready", "resT_copied", "hid_ready", "hid_act",
                                  "out_ready", "y_done", "var_ready_d", "rstd_ready_d", "fin_ready"))
            block = dctx.enter_context(nc.Block())

            @block.sync
            def _(sp):
                def load(b):
                    for dst, src in ((x1_in, x1_rows), (agg_in, agg_rows)):
                        sp.dma_start(dst[b % 2][:], src[b * N:(b + 1) * N, :].rearrange("(t p) c -> p t c", p=P)).then_inc(
                            in_loaded[b % 2], 16)

                load(0)
                for b in range(B):
                    if b + 1 < B:
                        if b >= 1:
                            sp.wait_ge(in_used, b)
                        load(b + 1)
                    sp.wait_ge(fin_ready, b + 1)
                    sp.dma_start(out[b].rearrange("(t p) c -> p t c", p=P), fin[b % 2][:]).then_inc(fin_stored[b % 2], 16)
                for q in range(2):
                    sp.wait_ge(fin_stored[q], 16 * (B // 2))

            @block.tensor
            def _(pe):
                for b in range(B):
                    pe.wait_ge(res_ready, b + 1)
                    for t in range(T):
                        mm = nc.tensor.transpose(resT_ps[:, bass.ts(t, P)], res[:, t, :], ident[:])
                    mm.then_inc(resT_ready, 1)
                    pe.wait_ge(resT_copied, b + 1)
                    for h in range(2):
                        mm = nc.tensor.matmul(hid_ps[:, bass.ts(h, 512)], W1_sb[:], resT[:, bass.ts(h, 512)],
                                              start=True, stop=True)
                    mm.then_inc(hid_ready, 1)
                    pe.wait_ge(hid_act, b + 1)
                    if b:
                        pe.wait_ge(y_done, b)
                    for t in range(T):
                        mm = nc.tensor.matmul(out_ps[:, t, :], hidT[:, bass.ts(t, P)], W2_sb[:], start=True, stop=True)
                    mm.then_inc(out_ready, 1)

            @block.scalar
            def _(act):
                for b in range(B):
                    act.wait_ge(resT_ready, b + 1)
                    nc.scalar.copy(resT[:], resT_ps[:]).then_inc(resT_copied, 1)
                    act.wait_ge(hid_ready, b + 1)
                    nc.scalar.activation(hidT[:], hid_ps[:], ACT.Relu, bias=b1_sb[:, 0:1]).then_inc(hid_act, 1)

            @block.gpsimd
            def _(pool):
                for b in range(B):
                    pool.wait_ge(var_ready, b + 1)
                    nc.gpsimd.tensor_tensor(rstd[:], var[:], power[:], ALU.pow).then_inc(rstd_ready, 1)

            @block.vector
            def _(dve):
                v = nc.vector
                count = [0]

                def done(*instructions):
                    for i in instructions:
                        i.then_inc(step, 1)
                    count[0] += len(instructions)
                    dve.wait_ge(step, count[0])

                def wide(ap):
                    return ap.unsqueeze(2).to_broadcast([P, T, C])

                def make_res(b):
                    dve.wait_ge(in_loaded[b % 2], 32 * (b // 2 + 1))
                    if b:
                        dve.wait_ge(resT_ready, b)
                    done(v.tensor_tensor(res[:], x1_in[b % 2][:], agg_in[b % 2][:], ALU.add))
                    dve.sem_inc(res_ready, 1)

                make_res(0)
                for b in range(B):
                    dve.wait_ge(out_ready, b + 1)
                    done(v.tensor_tensor(y[:], out_ps[:], b2_sb[:].unsqueeze(1).to_broadcast([P, T, C]), ALU.add))
                    dve.sem_inc(y_done, 1)
                    if b + 1 < B:
                        make_res(b + 1)
                    done(v.tensor_tensor(y[:], y[:], wide(mask_f[:, b * T:(b + 1) * T]), ALU.mult))
                    done(v.tensor_tensor(y[:], y[:], x1_in[b % 2][:], ALU.add))
                    dve.sem_inc(in_used, 1)
                    done(v.tensor_reduce(mean[:], y[:], AX_X, ALU.add))
                    done(v.tensor_scalar(mean[:], mean[:], 1.0 / C, None, ALU.mult))
                    done(v.tensor_tensor(cen[:], y[:], wide(mean[:]), ALU.subtract))
                    done(v.tensor_tensor(sq[:], cen[:], cen[:], ALU.mult))
                    done(v.tensor_reduce(var[:], sq[:], AX_X, ALU.add))
                    done(v.tensor_scalar(var[:], var[:], 1.0 / C, EPS, ALU.mult, ALU.add))
                    dve.sem_inc(var_ready, 1)
                    dve.wait_ge(rstd_ready, b + 1)
                    if b >= 2:
                        dve.wait_ge(fin_stored[b % 2], 16 * (b // 2))
                    done(v.tensor_tensor(fin[b % 2][:], cen[:], wide(rstd[:]), ALU.mult))
                    dve.sem_inc(fin_ready, 1)


def kernel(x, adj, nodemask, L0_gnn_weight, L0_gnn_bias, L1_gnn_W1, L1_gnn_b1, L1_gnn_W2, L1_gnn_b2):
    import numpy as np
    import concourse.bacc as bacc
    from concourse.bass_utils import run_bass_kernel_spmd

    x = np.asarray(x)
    adj = np.asarray(adj)
    mask = np.asarray(nodemask).view(np.uint8)
    w0 = np.asarray(L0_gnn_weight)
    C = x.shape[2]
    data = {
        "x": x,
        "xT": x.transpose(0, 2, 1),
        "adj": adj,
        "adjT": adj.transpose(0, 2, 1),
        "mask": mask.reshape(-1, P).T,
        "w_cat": w0[:, 0].transpose(1, 0, 2).reshape(C, -1),
        "bias0": np.asarray(L0_gnn_bias).reshape(-1),
        "W1": np.asarray(L1_gnn_W1),
        "b1": np.asarray(L1_gnn_b1).reshape(-1, 1),
        "W2": np.asarray(L1_gnn_W2),
        "b2": np.asarray(L1_gnn_b2).reshape(-1),
    }
    data = {f"in_{k}": np.ascontiguousarray(a) for k, a in data.items()}
    nc = bacc.Bacc("TRN2", target_bir_lowering=False, num_devices=1)
    args = [nc.dram_tensor(k, a.shape, mybir.dt.from_np(a.dtype), kind="ExternalInput").ap() for k, a in data.items()]
    out = nc.dram_tensor("out", x.shape, F32, kind="ExternalOutput").ap()
    build(nc, *args, out)
    result = run_bass_kernel_spmd(nc, [data], core_ids=[0])
    return result.results[0]["out"]
```

```python
from contextlib import ExitStack

import concourse.bass as bass
from concourse import mybir

F32 = mybir.dt.float32
F16 = mybir.dt.float16
BF16 = mybir.dt.bfloat16
I32 = mybir.dt.int32
U32 = mybir.dt.uint32
U8 = mybir.dt.uint8
ALU = mybir.AluOpType
ACT = mybir.ActivationFunctionType
AX_X = mybir.AxisListType.X

P = 128
EPS = 1e-5
T_THRESH = 10
TAUS = (0.25, 0.5, 0.75)
QWEIGHTS = (0.25, 0.5, 0.25)
PAD_VALUE = 1e30
FLOW = ((10, 1), (48, 1), (128, 1), (256, 4), (64, 1), (40, 1), (32, 1), (24, 1), (20, 1), (16, 1), (12, 1), (8, 1))
RARE = ((512, 8), (1024, 8))
LEVELS = FLOW + RARE
CAPS = sorted(cap for cap, _ in LEVELS)
MAX_FLOW = max(cap for cap, _ in FLOW)
FLOW_GROUPS = max(groups for _, groups in FLOW)
FLOW_FLOATS = 128 * 64
BLOCK = 64
META = 8
POSITION, PAD_ROW, NODE = 0, 3, 4


def for_tiles(eng, most, n, body, whole_fours=True):
    spans = [1]
    while spans[0] * 4 < most:
        spans.insert(0, spans[0] * 4)

    def nest(first, depth):
        with eng.Fori(0, 4 if depth else -(-most // spans[0])) as i:
            at = first + i * spans[depth]
            with eng.If(at < n):
                if spans[depth] == 1:
                    body(at)
                elif spans[depth] == 4 and whole_fours:
                    with eng.If(at + 3 < n):
                        with eng.Fori(0, 4) as k:
                            body(at + k)
                        eng.nop()
                    with eng.Else():
                        nest(at, depth + 1)
                    eng.nop()
                else:
                    nest(at, depth + 1)
                eng.nop()
            with eng.Else():
                eng.nop()
            eng.nop()

    nest(0, 0)


def sort_stages(n):
    p = 1
    while p < n:
        k = p
        while k >= 1:
            yield p, k
            k //= 2
        p *= 2


def windows(slots):
    runs = []
    for slot in slots:
        if runs and slot == runs[-1][0] + runs[-1][1]:
            runs[-1] = (runs[-1][0], runs[-1][1] + 1)
        else:
            runs.append((slot, 1))

    def group(items, span):
        out = []
        while items:
            (first, *rest), n, distance = items[0], 1, 0
            if len(items) > 1 and tuple(items[1][1:]) == tuple(rest):
                distance = items[1][0] - first
                if distance & (distance - 1) == 0 and first % distance + span(rest) <= distance:
                    while n < len(items) and items[n] == (first + n * distance, *rest):
                        n += 1
                else:
                    distance = 0
            out.append((first, n, distance, *rest))
            items = items[n:]
        return out

    return group(group(runs, lambda rest: rest[0]), lambda rest: (rest[0] - 1) * rest[1] + rest[2])


def sort_plan(low, cap):
    needed = set()
    for m in range(low + 1, cap + 1):
        for tau in TAUS:
            position = tau * (m - 1)
            needed |= {int(position), -int(-position // 1)}
    first, last = min(needed), max(needed)
    needed = set(range(first, last + 1))
    stages = []
    for p, k in reversed(list(sort_stages(cap))):
        edge = 0 if k == p else k
        pairs = [block + at + i for block in range(0, cap, 2 * p) for at in range(edge, 2 * p - edge, 2 * k)
                 for i in range(k) if at + i + k < 2 * p and block + at + i + k < cap]
        lows = [i for i in pairs if i in needed]
        highs = [i for i in pairs if i + k in needed]
        passing = needed - {i for i in pairs} - {i + k for i in pairs}
        ends = [[i for i in sorted(passing) if i % (2 * p) < p], [i for i in sorted(passing) if i % (2 * p) >= p]]
        cut = min([sorted(passing)], ends, key=lambda lists: sum(len(windows(part)) for part in lists))
        stages.insert(0, (k, lows, highs, cut))
        needed = passing | {i + d for i in lows + highs for d in (0, k)}
    return stages, first, last + 1


def below(cap):
    return max([c for c in CAPS if c < cap], default=0)


def build(nc, x, xT, adj, mask, w_cat, bias0, W1, b1, W2, b2, out):
    B, N, C = x.shape
    H = W1.shape[1]
    T = N // P
    NODES = B * N
    COLS = NODES // P
    K0 = w_cat.shape[1] // C

    ROW = N + 2 * META
    MOST_TILES = NODES * FLOW_GROUPS // P + len(FLOW) - 1
    TILES = MOST_TILES + 2
    LIST_COLS = NODES // P + 1
    COLUMNS = TILES + len(RARE) * LIST_COLS
    assert COLUMNS <= 512 and COLS % 4 == 0
    key_rows = nc.dram_tensor("key_rows", (NODES + 1, ROW), F16, kind="Internal").ap()
    x1_rows = nc.dram_tensor("x1_rows", (B * (N + 1), C), F32, kind="Internal").ap()
    agg_rows = nc.dram_tensor("agg_rows", (NODES, C), F32, kind="Internal").ap()
    rare_lists = nc.dram_tensor("rare_lists", (P, len(RARE) * LIST_COLS), I32, kind="Internal").ap()

    with ExitStack() as ctx:
        def sb(name, shape, dt):
            return ctx.enter_context(nc.sbuf_tensor(name, shape, dt))

        def ps(name, shape, dt=F32):
            return ctx.enter_context(nc.psum_tensor(name, shape, dt))

        def sem(name):
            return ctx.enter_context(nc.semaphore(name))

        ident = sb("ident", [P, P], F32)
        ident_b = sb("ident_b", [P, P], BF16)
        off_diag = sb("off_diag", [P, P], F16)
        before = sb("before", [P, P], BF16)
        ones = sb("ones", [P, P], F32)
        ones_b = sb("ones_b", [P, P], BF16)
        down = sb("down", [P, N], F16)
        up = sb("up", [P, N], F32)
        diag_key = sb("diag_key", [P, N], F16)
        ones_row = sb("ones_row", [P, N], F16)
        group_f = {g: sb(f"group_f{g}", [P, 1], F32) for g in sorted({g for _, g in LEVELS if g > 1})}
        lane_h = sb("lane_h", [P, P], F16)
        ramp_h = sb("ramp_h", [P, 512], F16)
        in_lanes = sb("in_lanes", [P, 1], F32)
        eps_t = sb("eps_t", [P, T], F32)
        power = sb("power", [P, T], F32)
        wcat_sb = sb("wcat_sb", [C, K0 * C], F32)
        bias0_sb = sb("bias0_sb", [P, C], F32)
        W1_sb = sb("W1_sb", [C, H], F32)
        b1_sb = sb("b1_sb", [H, 1], F32)
        W2_sb = sb("W2_sb", [H, C], F32)
        b2_sb = sb("b2_sb", [P, C], F32)
        mask_u = sb("mask_u", [P, COLS], U8)
        mask_f = sb("mask_f", [P, COLS], F32)
        m_all = sb("m_all", [P, COLS], F32)
        tiles_of = sb("tiles_of", [P, len(LEVELS) + 1], I32)

        slots = [sb(f"slots{i}", [P, T * N], F32) for i in range(2)]

        def rows(ap, first, n):
            return ap[first:first + n, :]

        step = sem("step")
        first_adj_loaded = sem("first_adj_loaded")
        adj_sb = slots[0][:].rearrange("p (t n) -> p t n", t=T)
        adjT_sb = slots[1][:].rearrange("p (t n) -> p t n", t=T)

        with ExitStack() as sctx:
            loaded = sctx.enter_context(nc.semaphore("weights_loaded"))
            iotas = sctx.enter_context(nc.semaphore("iotas_done"))
            consts = sctx.enter_context(nc.semaphore("consts_done"))
            pad_stored = sctx.enter_context(nc.semaphore("pad_stored"))

            def ssb(name, shape, dt):
                return sctx.enter_context(nc.sbuf_tensor(name, shape, dt))

            diff = ssb("diff", [P, P], I32)
            ramp_i = ssb("ramp_i", [P, N], I32)
            part_i = ssb("part_i", [P, 1], I32)
            group_i = {g: ssb(f"group_i{g}", [P, 1], I32) for g in group_f}
            lane_i = ssb("lane_i", [P, P], I32)
            pad_f = ssb("pad_f", [B, C], F32)
            pad_k = ssb("pad_k", [1, ROW], F16)
            pad_meta = pad_k[:, N:ROW].bitcast(F32)
            block = sctx.enter_context(nc.Block())

            @block.sync
            def _(sp):
                sp.dma_start(wcat_sb[:], w_cat).then_inc(loaded, 16)
                sp.dma_start(bias0_sb[:], bias0.partition_broadcast(P)).then_inc(loaded, 16)
                sp.dma_start(W1_sb[:], W1).then_inc(loaded, 16)
                sp.dma_start(b1_sb[:], b1).then_inc(loaded, 16)
                sp.dma_start(W2_sb[:], W2).then_inc(loaded, 16)
                sp.dma_start(b2_sb[:], b2.partition_broadcast(P)).then_inc(loaded, 16)
                sp.dma_start(mask_u[:], mask).then_inc(loaded, 16)
                sp.dma_start(adj_sb, adj[0].rearrange("(t p) n -> p t n", p=P)).then_inc(first_adj_loaded, 16)
                sp.wait_ge(consts, 1)
                sp.dma_start(x1_rows.rearrange("(b n) c -> b n c", b=B)[:, N, :], pad_f[:]).then_inc(pad_stored, 16)
                sp.dma_start(rows(key_rows, NODES, 1), pad_k[:]).then_inc(pad_stored, 16)
                sp.wait_ge(pad_stored, 32)
                sp.wait_ge(loaded, 16 * 7)

            @block.gpsimd
            def _(pool):
                nc.gpsimd.iota(diff[:], pattern=[[1, P]], base=0, channel_multiplier=-1).then_inc(iotas, 1)
                nc.gpsimd.iota(ramp_i[:], pattern=[[1, N]], base=0, channel_multiplier=0).then_inc(iotas, 1)
                nc.gpsimd.iota(part_i[:], pattern=[[0, 1]], base=0, channel_multiplier=1).then_inc(iotas, 1)

            @block.vector
            def _(dve):
                count = [0]

                def done(*instructions):
                    for i in instructions:
                        i.then_inc(step, 1)
                    count[0] += len(instructions)
                    dve.wait_ge(step, count[0])

                dve.wait_ge(iotas, 3)
                dve.wait_ge(loaded, 16 * 7)
                v = nc.vector
                done(
                    v.tensor_scalar(ident[:], diff[:], 0, None, ALU.is_equal),
                    v.tensor_scalar(ident_b[:], diff[:], 0, None, ALU.is_equal),
                    v.tensor_scalar(off_diag[:], diff[:], 0, None, ALU.not_equal),
                    v.tensor_scalar(before[:], diff[:], 0, None, ALU.is_gt),
                    v.memset(ones[:], 1.0),
                    v.memset(ones_b[:], 1.0),
                    v.memset(ones_row[:], 1.0),
                    v.memset(eps_t[:], EPS),
                    v.memset(power[:], -0.5),
                    v.memset(pad_f[:], PAD_VALUE),
                    v.memset(pad_k[:], 0.0),
                    v.tensor_scalar(down[:], ramp_i[:], -1.0, float(N), ALU.mult, ALU.add),
                    v.tensor_copy(up[:], ramp_i[:]),
                    v.tensor_scalar(lane_i[:], ramp_i[:, 0:P], P // FLOW_GROUPS - 1, None, ALU.bitwise_and),
                    v.tensor_scalar(in_lanes[:], part_i[:], float(P // FLOW_GROUPS), None, ALU.is_lt),
                    *[v.tensor_scalar(group_i[g][:], part_i[:], (P // g).bit_length() - 1, None,
                                      ALU.logical_shift_right) for g in group_i],
                    v.tensor_copy(mask_f[:], mask_u[:]),
                )
                done(*[v.tensor_copy(group_f[g][:], group_i[g][:]) for g in group_i],
                     v.tensor_copy(lane_h[:], lane_i[:]), v.tensor_copy(ramp_h[:], ramp_i[:, 0:512]),
                     v.memset(pad_meta[:, PAD_ROW:PAD_ROW + 1], float(B * (N + 1) - 1)),
                     v.memset(pad_meta[:, NODE:NODE + 1], float(NODES)),
                     *[v.tensor_tensor(diag_key[:, bass.ts(t, P)], down[:, bass.ts(t, P)], ident_b[:], ALU.mult)
                       for t in range(T)])
                dve.sem_inc(consts, 1)
                dve.sem_clear(step)

        with ExitStack() as actx:
            def asb(name, shape, dt):
                return actx.enter_context(nc.sbuf_tensor(name, shape, dt))

            def apsum(name, shape, dt=F32):
                return actx.enter_context(nc.psum_tensor(name, shape, dt))

            ON_VECTOR = T - 3
            x_sb = asb("x_sb", [P, T, C], F32)
            xT_sb = asb("xT_sb", [C, N], F32)
            nb = asb("nb", [P, T, N], F16)
            nbkey = asb("nbkey", [P, T, N], F16)
            ranked = asb("ranked", [P, T, N], F16)
            removed = asb("removed", [P, T, N], BF16)
            key_out = asb("key_out", [P, T, N], F16)
            rank = asb("rank", [P, N], F16)
            off_middle = asb("off_middle", [P, 2, N], F16)
            positive = asb("positive", [P, N], BF16)
            act_junk = asb("act_junk", [P, N], BF16)
            deg = asb("deg", [P, T], F32)
            safe_deg = asb("safe_deg", [P, T], F32)
            dpow = asb("dpow", [P, T], F32)
            dsc = asb("dsc", [P, T], F32)
            dsc_twice = asb("dsc_twice", [P, T], F32)
            dsc_square = asb("dsc_square", [P, T], F32)
            keep = asb("keep", [P, T], F32)
            m_batch = asb("m_batch", [P, T], F32)
            nb_count = asb("nb_count", [P, T], F32)
            count_i = asb("count_i", [P, T], I32)
            skip_f = asb("skip_f", [P, T], F32)
            middle = asb("middle", [P, T], F32)
            half_skip = asb("half_skip", [P, T], F32)
            dil = asb("dil", [P, T], F32)
            mask_b = asb("mask_b", [P, T], F32)
            proj = asb("proj", [P, T, K0 * C], F32)
            z = asb("z", [P, T, C], F32)
            yT_sb = asb("yT_sb", [C, N], F32)
            bb = [asb(f"bb{i}", [P, T, C], F32) for i in range(3)]
            tmp = asb("tmp", [P, T, C], F32)
            tmp2 = asb("tmp2", [P, T, C], F32)
            mean = asb("mean", [P, T], F32)
            var = asb("var", [P, T], F32)
            rstd = asb("rstd", [P, T], F32)
            x1_sb = asb("x1_sb", [P, T, C], F32)

            wide_ps = apsum("wide_ps", [P, N])
            y_ps = apsum("y_ps", [P, T, C])
            pair_ps = [apsum(f"pair_ps{i}", [P, N]) for i in range(2)]

            names = ("adj_loaded adj_for_pe adj_for_act adj_for_dve adj_free x_loaded x_for_pe x_for_dve x_free "
                     "deg_ready safe_ready pow_ready var_ready rstd_ready half_projected half_copied proj_ready "
                     "z_ready yT_ready yT_copied y_ready y_free nb_ready nb_free middle_ready removed_ready "
                     "turned0 turned1 off0 off1 off_free0 off_free1 pair_free0 pair_free1 rem_ready0 rem_ready1 "
                     "key_ready keys_for_act0 keys_for_act1 keys_for_act2 keys_for_act3 keys_counted keys_stored "
                     "x1_ready x1_stored").split()
            s = {n: actx.enter_context(nc.semaphore(n)) for n in names}
            act_step = actx.enter_context(nc.semaphore("act_step"))
            block = actx.enter_context(nc.Block())

            def take(eng, name, n=1):
                eng.wait_ge(s[name], n)
                eng.sem_clear(s[name])

            def each_batch(eng, body):
                with eng.Fori(0, B - 1) as b:
                    body(b, True)
                body(B - 1, False)

            @block.sync
            def _(sp):
                def load_adj(b):
                    sp.dma_start(adj_sb, adj[bass.ds(b, 1)].rearrange("o (t p) n -> p (o t) n", p=P)).then_inc(
                        s["adj_loaded"], 16)

                def load_x(b):
                    sp.dma_start(x_sb[:], x[bass.ds(b, 1)].rearrange("o (t p) c -> p (o t) c", p=P)).then_inc(
                        s["x_loaded"], 16)
                    sp.dma_start(xT_sb[:], xT[bass.ds(b, 1)].rearrange("o c n -> (o c) n")).then_inc(s["x_loaded"], 16)

                def adj_landed():
                    sp.sem_inc(s["adj_for_pe"], 1)
                    sp.sem_inc(s["adj_for_act"], 1)
                    sp.sem_inc(s["adj_for_dve"], 1)

                def x_landed():
                    take(sp, "x_loaded", 32)
                    sp.sem_inc(s["x_for_pe"], 1)
                    sp.sem_inc(s["x_for_dve"], 1)

                def turn(b, more):
                    if more:
                        take(sp, "adj_free", 3)
                        load_adj(b + 1)
                        take(sp, "adj_loaded", 16)
                        adj_landed()
                        take(sp, "x_free", 2)
                        load_x(b + 1)
                        x_landed()
                    take(sp, "key_ready")
                    sp.dma_start(key_rows[bass.ds(b * N, N), 0:N].rearrange("(t p) n -> p t n", p=P),
                                 key_out[:]).then_inc(s["keys_stored"], 16)
                    take(sp, "x1_ready")
                    sp.dma_start(x1_rows[bass.ds(b * (N + 1), N)].rearrange("(t p) c -> p t c", p=P),
                                 x1_sb[:]).then_inc(s["x1_stored"], 16)

                load_x(0)
                sp.wait_ge(first_adj_loaded, 16)
                adj_landed()
                x_landed()
                each_batch(sp, turn)

            @block.scalar
            def _(act):
                a = nc.scalar

                def finish(instruction):
                    instruction.then_inc(act_step, 1)
                    act.wait_ge(act_step, 1)
                    act.sem_clear(act_step)

                def scan_tile(t):
                    finish(a.activation(act_junk[:], adj_sb[:, t, :], ACT.Copy, accum_out=deg[:, t:t + 1]))
                    if t >= T - ON_VECTOR:
                        return
                    finish(a.activation(positive[:], adj_sb[:, t, :], ACT.Relu))
                    finish(a.activation(nb[:, t, :], positive[:], ACT.Sign))

                def scanned():
                    act.sem_inc(s["adj_free"], 1)
                    act.sem_inc(s["deg_ready"], 1)
                    act.sem_inc(s["nb_ready"], 1)

                def move_product():
                    take(act, "yT_ready")
                    a.copy(yT_sb[:], wide_ps[0:C, :]).then_inc(s["yT_copied"], 1)

                def turn(b, more):
                    for t in range(T):
                        if t in (0, 2):
                            take(act, "half_projected")
                            finish(a.copy(proj[:, bass.ts(t // 2, T // 2), :],
                                          wide_ps[:].rearrange("p (t k) -> p t k", t=T // 2)))
                            act.sem_inc(s["half_copied"], 1)
                            if t:
                                act.sem_inc(s["proj_ready"], 1)
                        take(act, f"turned{t % 2}")
                        a.copy(adjT_sb[:, :, bass.ts(t, P)],
                               pair_ps[t % 2][:].rearrange("p (j n) -> p j n", j=T)).then_inc(
                            s[f"pair_free{t % 2}"], 1)
                    move_product()
                    take(act, "middle_ready")
                    for t in range(T):
                        take(act, f"off_free{t % 2}")
                        a.activation(off_middle[:, t % 2, :], ranked[:, t, :], ACT.Abs,
                                     bias=middle[:, t:t + 1]).then_inc(s[f"off{t % 2}"], 1)
                    move_product()
                    if more:
                        take(act, "adj_for_act")
                        take(act, "nb_free")
                        for t in range(T):
                            scan_tile(t)
                        scanned()
                    for t in range(T):
                        if t % 2 == 0:
                            take(act, f"keys_for_act{t // 2}")
                        if t == T - 2:
                            move_product()
                        finish(a.activation(act_junk[:], key_out[:, t, :], ACT.Sign, accum_out=m_batch[:, t:t + 1]))
                    act.sem_inc(s["keys_counted"], 1)
                    finish(a.copy(m_all[:, bass.ds(b * T, T)], m_batch[:]))

                take(act, "adj_for_act")
                for t in range(T):
                    scan_tile(t)
                scanned()
                each_batch(act, turn)

            @block.gpsimd
            def _(pool):
                with pool.Fori(0, B):
                    take(pool, "safe_ready")
                    nc.gpsimd.tensor_tensor(dpow[:], safe_deg[:], power[:], ALU.pow).then_inc(s["pow_ready"], 1)
                    take(pool, "var_ready")
                    nc.gpsimd.tensor_tensor(rstd[:], var[:], power[:], ALU.pow).then_inc(s["rstd_ready"], 1)

            @block.tensor
            def _(pe):
                def project(h):
                    for u in range(T // 2):
                        mm = nc.tensor.matmul(wide_ps[:, bass.ts(u, K0 * C)], xT_sb[:, bass.ts(h * T // 2 + u, P)],
                                              wcat_sb[:], start=True, stop=True)
                    mm.then_inc(s["half_projected"], 1)

                def product_part(j):
                    for g in range(2):
                        mm = nc.tensor.matmul(wide_ps[0:C, bass.ts(g, 512)], z[:, j, :], adjT_sb[:, j, bass.ts(g, 512)],
                                              start=(j == 0), stop=(j == T - 1))
                    return mm

                def turn_back(mm):
                    mm.then_inc(s["yT_ready"], 1)
                    take(pe, "yT_copied")
                    take(pe, "y_free")
                    for t in range(T):
                        mm = nc.tensor.transpose(y_ps[:, t, :], yT_sb[:, bass.ts(t, P)], ident[0:C, 0:C])
                    mm.then_inc(s["y_ready"], 1)

                def mirror(t):
                    q = t % 2
                    take(pe, f"pair_free{q}")
                    for g in range(2):
                        half = pair_ps[q][:, bass.ts(g, 512)]
                        nc.tensor.matmul(half, ident_b[:], removed[:, t, bass.ts(g, 512)], start=True, stop=False)
                        for j in range(4):
                            mm = nc.tensor.matmul(half[:, bass.ts(j, P)], removed[:, g * 4 + j, bass.ts(t, P)],
                                                  ident_b[:], start=False, stop=(j == 3))
                    mm.then_inc(s[f"rem_ready{q}"], 1)

                def turn(b, more):
                    take(pe, "x_for_pe")
                    project(0)
                    take(pe, "adj_for_pe")
                    for t in range(T):
                        if t == 2:
                            take(pe, "half_copied")
                            project(1)
                            pe.sem_inc(s["x_free"], 1)
                        take(pe, f"pair_free{t % 2}")
                        for j in range(T):
                            mm = nc.tensor.transpose(pair_ps[t % 2][:, bass.ts(j, P)], adj_sb[:, t, bass.ts(j, P)],
                                                     ident[:])
                        mm.then_inc(s[f"turned{t % 2}"], 1)
                    take(pe, "half_copied")
                    for q in range(2):
                        take(pe, f"pair_free{q}")
                    pe.sem_inc(s["adj_free"], 1)
                    for q in range(2):
                        pe.sem_inc(s[f"pair_free{q}"], 1)
                    take(pe, "z_ready")
                    for j in range(T):
                        mm = product_part(j)
                    turn_back(mm)
                    take(pe, "z_ready")
                    for j in range(T):
                        mm = product_part(j)
                    turn_back(mm)
                    take(pe, "removed_ready")
                    mirror(0)
                    mirror(1)
                    take(pe, "z_ready")
                    for j in range(T):
                        mm = product_part(j)
                        if j + 2 < T:
                            mirror(j + 2)
                    turn_back(mm)

                for q in range(2):
                    pe.sem_inc(s[f"pair_free{q}"], 1)
                each_batch(pe, turn)

            @block.vector
            def _(dve):
                v = nc.vector
                count = [0]

                def done(*instructions):
                    for i in instructions:
                        i.then_inc(step, 1)
                    count[0] += len(instructions)
                    dve.wait_ge(step, count[0])

                def wide(ap):
                    return ap.unsqueeze(2).to_broadcast([P, T, C])

                def apply_laplacian(src, add_to, factor, minus, dst, scale, z_scale):
                    done(v.tensor_tensor(tmp2[:], src, wide(keep[:]), ALU.mult))
                    done(v.scalar_tensor_tensor(out=dst, in0=tmp2[:], scalar=factor, in1=add_to, op0=ALU.mult,
                                                op1=ALU.add))
                    if minus is not None:
                        done(v.tensor_tensor(dst, dst, minus, ALU.subtract))
                    if z_scale is not None:
                        done(v.tensor_tensor(tmp2[:], dst, wide(dsc[:]), ALU.mult))
                    take(dve, "y_ready")
                    if z_scale is not None:
                        done(v.tensor_tensor(tmp[:], y_ps[:], wide(z_scale[:]), ALU.mult))
                        done(v.tensor_tensor(z[:], tmp2[:], tmp[:], ALU.subtract))
                        dve.sem_inc(s["z_ready"], 1)
                    done(v.tensor_tensor(tmp[:], y_ps[:], wide(scale[:]), ALU.mult))
                    dve.sem_inc(s["y_free"], 1)
                    done(v.tensor_tensor(dst, dst, tmp[:], ALU.subtract))

                def look_at(t):
                    return v.tensor_scalar(nb[:, t, :], adj_sb[:, t, :], 0.0, None, ALU.is_gt)

                def order(k):
                    return proj[:, :, k * C:(k + 1) * C]

                def turn(b, more):
                    dve.sem_clear(step)
                    count[0] = 0
                    take(dve, "deg_ready")
                    done(v.tensor_scalar(safe_deg[:], deg[:], 1e-37, None, ALU.max),
                         v.tensor_scalar(keep[:], deg[:], 0.0, None, ALU.not_equal),
                         v.tensor_scalar(dsc[:], deg[:], 0.0, None, ALU.is_gt))
                    dve.sem_inc(s["safe_ready"], 1)
                    take(dve, "nb_ready")
                    for t in range(T):
                        done(v.tensor_tensor(nb[:, t, bass.ts(t, P)], nb[:, t, bass.ts(t, P)], off_diag[:], ALU.mult))
                        done(v.tensor_tensor_scan(rank[:], ones_row[:], nb[:, t, :], 0.0, ALU.mult, ALU.add),
                             v.tensor_tensor(nbkey[:, t, :], nb[:, t, :], down[:], ALU.mult))
                        done(v.tensor_tensor(ranked[:, t, :], rank[:], nb[:, t, :], ALU.mult),
                             v.tensor_copy(nb_count[:, t:t + 1], rank[:, N - 1:N]))
                        if t == 0:
                            take(dve, "pow_ready")
                            take(dve, "proj_ready")
                            done(v.tensor_tensor(dsc[:], dsc[:], dpow[:], ALU.mult))
                            done(v.tensor_tensor(z[:], order(3), wide(dsc[:]), ALU.mult),
                                 v.tensor_scalar(dsc_twice[:], dsc[:], 2.0, None, ALU.mult))
                            dve.sem_inc(s["z_ready"], 1)
                            done(v.tensor_tensor(dsc_square[:], dsc_twice[:], dsc[:], ALU.mult))
                        if t == T - 2:
                            apply_laplacian(order(3), order(2), 2.0, None, bb[0][:], dsc_twice, dsc_square)
                    if more:
                        dve.sem_inc(s["nb_free"], 1)
                    done(v.tensor_scalar(count_i[:], nb_count[:], 1.0, None, ALU.add),
                         v.tensor_copy(mask_b[:], mask_f[:, bass.ds(b * T, T)]),
                         v.tensor_scalar(dil[:], nb_count[:], float(T_THRESH), None, ALU.is_gt))
                    done(v.tensor_scalar(count_i[:], count_i[:], 1, None, ALU.logical_shift_right),
                         v.tensor_tensor(dil[:], dil[:], mask_b[:], ALU.mult))
                    done(v.tensor_copy(skip_f[:], count_i[:]))
                    done(v.tensor_scalar(middle[:], skip_f[:], -1.5, None, ALU.mult),
                         v.tensor_scalar(half_skip[:], skip_f[:], 0.5, 1.0, ALU.mult, ALU.add))
                    dve.sem_inc(s["middle_ready"], 1)
                    done(v.tensor_tensor(half_skip[:], half_skip[:], dil[:], ALU.mult))
                    done(v.tensor_scalar(half_skip[:], half_skip[:], -1.0, None, ALU.add))
                    take(dve, "x_for_dve")
                    if more:
                        take(dve, "adj_for_dve")

                    def step_between(t):
                        if t == 0:
                            return [v.tensor_tensor(tmp2[:], order(0), bb[0][:], ALU.subtract)]
                        if t == 1:
                            return [v.tensor_tensor(tmp2[:], tmp2[:], x_sb[:], ALU.add)]
                        if t == 2:
                            return [v.tensor_tensor(bb[2][:], tmp2[:], bias0_sb[:].unsqueeze(1).to_broadcast([P, T, C]),
                                                    ALU.add)]
                        return [look_at(t)] if more else []

                    for t in range(T):
                        take(dve, f"off{t % 2}")
                        done(v.tensor_scalar(removed[:, t, :], off_middle[:, t % 2, :], half_skip[:, t:t + 1], None,
                                             ALU.is_equal))
                        dve.sem_inc(s[f"off_free{t % 2}"], 1)
                        done(*step_between(t))
                    dve.sem_inc(s["removed_ready"], 1)
                    dve.sem_inc(s["x_free"], 1)
                    if more:
                        dve.sem_inc(s["adj_free"], 1)
                    apply_laplacian(bb[0][:], order(1), 2.0, order(3), bb[1][:], dsc_twice, dsc_square)
                    take(dve, "keys_stored", 16)
                    take(dve, "keys_counted")
                    for t in range(T):
                        take(dve, f"rem_ready{t % 2}")
                        done(v.scalar_tensor_tensor(out=key_out[:, t, :], in0=pair_ps[t % 2][:], scalar=0.0,
                                                    in1=nbkey[:, t, :], op0=ALU.is_equal, op1=ALU.mult))
                        dve.sem_inc(s[f"pair_free{t % 2}"], 1)
                        done(v.tensor_tensor(key_out[:, t, bass.ts(t, P)], key_out[:, t, bass.ts(t, P)],
                                             diag_key[:, bass.ts(t, P)], ALU.add))
                        if t % 2:
                            dve.sem_inc(s[f"keys_for_act{t // 2}"], 1)
                    dve.sem_inc(s["key_ready"], 1)
                    apply_laplacian(bb[1][:], bb[2][:], 1.0, None, bb[0][:], dsc, None)
                    done(v.tensor_reduce(mean[:], bb[0][:], AX_X, ALU.add))
                    done(v.tensor_scalar(mean[:], mean[:], 1.0 / C, None, ALU.mult))
                    done(v.tensor_tensor(bb[1][:], bb[0][:], wide(mean[:]), ALU.subtract))
                    done(v.tensor_tensor(tmp[:], bb[1][:], bb[1][:], ALU.mult))
                    done(v.tensor_reduce(var[:], tmp[:], AX_X, ALU.add))
                    done(v.tensor_scalar(var[:], var[:], 1.0 / C, EPS, ALU.mult, ALU.add))
                    dve.sem_inc(s["var_ready"], 1)
                    take(dve, "rstd_ready")
                    take(dve, "x1_stored", 16)
                    done(v.tensor_tensor(x1_sb[:], bb[1][:], wide(rstd[:]), ALU.mult))
                    dve.sem_inc(s["x1_ready"], 1)

                for q in range(2):
                    dve.sem_inc(s[f"off_free{q}"], 1)
                dve.sem_inc(s["keys_counted"], 1)
                dve.sem_inc(s["y_free"], 1)
                dve.sem_inc(s["keys_stored"], 16)
                dve.sem_inc(s["x1_stored"], 16)
                count[0] = 0
                take(dve, "adj_for_dve")
                done(*[look_at(t) for t in range(T - ON_VECTOR, T)])
                dve.sem_inc(s["adj_free"], 1)
                each_batch(dve, turn)
                dve.sem_clear(step)
                take(dve, "keys_stored", 16)
                take(dve, "x1_stored", 16)

        nodes_at = sb("nodes_at", [P, 514], I32)

        with ExitStack() as bctx:
            def bsb(name, shape, dt):
                return bctx.enter_context(nc.sbuf_tensor(name, shape, dt))

            def bsem(name):
                return bctx.enter_context(nc.semaphore(name))

            NL = len(LEVELS)
            AT_ONCE = 4
            meta = bsb("meta", [P, COLS, META], F32)
            at_level = bsb("at_level", [P, NL, COLS], F32)
            at_level_b = bsb("at_level_b", [P, NL, COLS], BF16)
            ahead = bsb("ahead", [P, NL, COLS], F32)
            here = bsb("here", [P, NL, COLS], F32)
            earlier = bsb("earlier", [P, NL, COLS], F32)
            order_i = bsb("order_i", [P, NL, COLS], I32)
            slot_i = bsb("slot_i", [P, NL, COLS], I32)
            part = bsb("part", [P, NL, COLS], F32)
            slot_at = bsb("slot_at", [P, NL, COLS], F32)
            column = bsb("column", [P, COLS], F32)
            slot = {g: bsb(f"slot{g}", [P, COLS], F32) for g in (1, FLOW_GROUPS)}
            fill_up = bsb("fill_up", [P, NL], F32)
            total_i = bsb("total_i", [P, NL], I32)
            total = bsb("total", [P, NL], F32)
            tiles_end = bsb("tiles_end", [P, NL], F32)
            first_column = bsb("first_column", [P, NL], F32)
            node_i = bsb("node_i", [P, COLS], I32)
            batch_i = bsb("batch_i", [P, COLS], I32)
            part_f = bsb("part_f", [P, 1], F32)
            hit_one = bsb("hit_one", [P, AT_ONCE, P], F16)
            to_slot = bsb("to_slot", [P, 2, AT_ONCE, P], F16)
            slot_weights = bsb("slot_weights", [P, 2, AT_ONCE, 2, P], F16)
            to_column = bsb("to_column", [P, 2, AT_ONCE, COLUMNS], F16)
            count_ps = bctx.enter_context(nc.psum_tensor("count_ps", [P, 2, 1024], F32))
            table_ps = bctx.enter_context(nc.psum_tensor("table_ps", [P, 512], F32))
            records_ready, nodes_ready, counted, level_ready, stored, slots_ready, hot, used = (
                bsem(n) for n in ("records_ready", "nodes_ready", "counted", "level_ready", "records_stored",
                                  "slots_ready", "one_hots_ready", "one_hots_used"))
            block = bctx.enter_context(nc.Block())

            @block.sync
            def _(sp):
                sp.wait_ge(records_ready, 1)
                sp.dma_start(key_rows[0:NODES, N:ROW].rearrange("(c p) k -> p c k", p=P),
                             meta[:].rearrange("p c k -> p (c k)").bitcast(F16).rearrange(
                                 "p (c k) -> p c k", c=COLS)).then_inc(stored, 16)
                sp.wait_ge(stored, 16)

            @block.gpsimd
            def _(pool):
                nc.gpsimd.iota(node_i[:], pattern=[[P, COLS]], base=0, channel_multiplier=1).then_inc(nodes_ready, 1)

            @block.scalar
            def _(act):
                for turn in range(COLS // AT_ONCE):
                    act.wait_ge(slots_ready, turn + 1)
                    if turn >= 2:
                        act.wait_ge(used, turn - 1)
                    q = turn % 2
                    for i in range(AT_ONCE):
                        nc.scalar.activation(slot_weights[:, q, i, 0, :], to_slot[:, q, i, :], ACT.Copy,
                                             scale=float((turn * AT_ONCE + i - COLS) * P)).then_inc(hot, 1)
                    nc.scalar.activation(slot_weights[:, q, :, 1, :], to_slot[:, q, :, :], ACT.Copy,
                                         scale=part_f[:, 0:1]).then_inc(hot, 1)

            @block.tensor
            def _(pe):
                pe.wait_ge(level_ready, 1)
                flat = at_level_b[:].rearrange("p l c -> p (l c)")
                for g in range(2):
                    lhs = (before, ones_b)[g]
                    for first in range(0, NL * COLS, 512):
                        n = min(512, NL * COLS - first)
                        mm = nc.tensor.matmul(count_ps[:, g, first:first + n], lhs[:], flat[:, first:first + n],
                                              start=True, stop=True)
                mm.then_inc(counted, 1)
                for turn in range(COLS // AT_ONCE):
                    pe.wait_ge(hot, (turn + 1) * (AT_ONCE + 1))
                    for i in range(AT_ONCE):
                        for part_ in range(2):
                            first = turn == 0 and i == 0 and part_ == 0
                            last = turn == COLS // AT_ONCE - 1 and i == AT_ONCE - 1 and part_ == 1
                            mm = nc.tensor.matmul(table_ps[:, 0:COLUMNS], slot_weights[:, turn % 2, i, part_, :],
                                                  to_column[:, turn % 2, i, :], start=first, stop=last)
                    mm.then_inc(used, 1)

            @block.vector
            def _(dve):
                v = nc.vector
                count = [0]

                def done(*instructions):
                    for i in instructions:
                        i.then_inc(step, 1)
                    count[0] += len(instructions)
                    dve.wait_ge(step, count[0])

                done(v.memset(meta[:], 0.0), v.memset(first_column[:], 0.0),
                     *[v.memset(fill_up[:, i:i + 1], float(P // groups - 1)) for i, (_, groups) in enumerate(LEVELS)],
                     *[v.tensor_scalar(at_level[:, i, :], m_all[:], float(cap), None, ALU.is_le)
                       for i, (cap, _) in enumerate(LEVELS)])
                done(*[v.scalar_tensor_tensor(out=at_level[:, i, :], in0=m_all[:], scalar=float(below(cap)),
                                              in1=at_level[:, i, :], op0=ALU.is_gt, op1=ALU.mult)
                       for i, (cap, _) in enumerate(LEVELS)])
                done(v.tensor_copy(at_level_b[:], at_level[:]))
                dve.sem_inc(level_ready, 1)
                dve.wait_ge(nodes_ready, 1)
                shift = N.bit_length() - 1
                done(*[v.tensor_scalar(meta[:, :, POSITION + i], m_all[:], -1.0, -tau, ALU.add, ALU.mult)
                       for i, tau in enumerate(TAUS)],
                     v.tensor_scalar(batch_i[:], node_i[:], shift, None, ALU.logical_shift_right),
                     v.tensor_copy(meta[:, :, NODE], node_i[:]), v.tensor_copy(part_f[:], node_i[:, 0:1]))
                done(v.tensor_scalar(meta[:, :, PAD_ROW], batch_i[:], float(N + 1), float(N), ALU.mult, ALU.add))
                dve.sem_inc(records_ready, 1)
                dve.wait_ge(counted, 1)
                done(v.tensor_copy(earlier[:].rearrange("p l c -> p (l c)"), count_ps[:, 0, 0:NL * COLS]),
                     v.tensor_copy(here[:].rearrange("p l c -> p (l c)"), count_ps[:, 1, 0:NL * COLS]))
                done(*[v.tensor_tensor_scan(ahead[:, i, :], ones[:, 0:COLS], here[:, i, :], 0.0, ALU.mult, ALU.add)
                       for i in range(NL)],
                     v.tensor_tensor(part[:], earlier[:], here[:], ALU.subtract))
                done(v.tensor_tensor(order_i[:], ahead[:], part[:], ALU.add),
                     v.tensor_tensor(total_i[:], ahead[:, :, COLS - 1], fill_up[:], ALU.add))
                tile_bits = [(P // groups).bit_length() - 1 for _, groups in LEVELS]
                slot_bits = tile_bits[0:len(FLOW)] + [P.bit_length() - 1] * len(RARE)
                done(*[v.tensor_scalar(slot_i[:, i, :], order_i[:, i, :], (1 << slot_bits[i]) - 1, None,
                                       ALU.bitwise_and) for i in range(NL)],
                     *[v.tensor_scalar(total_i[:, i:i + 1], total_i[:, i:i + 1], tile_bits[i], None,
                                       ALU.logical_shift_right) for i in range(NL)])
                done(*[v.tensor_scalar(order_i[:, i, :], order_i[:, i, :], slot_bits[i], None,
                                       ALU.logical_shift_right) for i in range(NL)],
                     v.tensor_copy(slot_at[:], slot_i[:]), v.tensor_copy(total[:], total_i[:]))
                flow = slice(0, len(FLOW))
                done(v.tensor_scalar(total[:, flow], total[:, flow], 1.0, None, ALU.max),
                     v.tensor_copy(part[:], order_i[:]),
                     v.tensor_scalar(slot_at[:], slot_at[:], 1.0, None, ALU.add))
                done(v.tensor_tensor_scan(tiles_end[:], ones[:, 0:NL], total[:], 0.0, ALU.mult, ALU.add),
                     v.tensor_tensor(slot_at[:], slot_at[:], at_level[:], ALU.mult))
                done(v.tensor_tensor(first_column[:, flow], tiles_end[:, flow], total[:, flow], ALU.subtract),
                     *[v.memset(first_column[:, i:i + 1], float(TILES + (i - len(FLOW)) * LIST_COLS))
                       for i in range(len(FLOW), NL)],
                     v.tensor_copy(tiles_of[:, 0:NL], total[:]),
                     v.tensor_copy(tiles_of[:, NL:NL + 1], tiles_end[:, len(FLOW) - 1:len(FLOW)]))
                done(v.tensor_tensor(part[:], part[:], first_column[:].unsqueeze(2).to_broadcast([P, NL, COLS]),
                                     ALU.add))
                done(v.tensor_tensor(part[:], part[:], at_level[:], ALU.mult))
                narrow = [g for _, g in FLOW].index(FLOW_GROUPS)
                done(v.tensor_reduce(column[:], part[:].rearrange("p l c -> p c l"), AX_X, ALU.add),
                     v.tensor_reduce(slot[1][:], slot_at[:].rearrange("p l c -> p c l"), AX_X, ALU.add))
                done(v.tensor_tensor(slot[1][:], slot[1][:], slot_at[:, narrow, :], ALU.subtract),
                     v.tensor_scalar(slot[FLOW_GROUPS][:], slot_at[:, narrow, :], -1.0, None, ALU.add))
                done(v.tensor_scalar(slot[1][:], slot[1][:], -1.0, None, ALU.add))
                for turn in range(COLS // AT_ONCE):
                    if turn >= 2:
                        dve.wait_ge(used, turn - 1)
                    q = turn % 2
                    columns = range(turn * AT_ONCE, (turn + 1) * AT_ONCE)
                    done(*[v.tensor_scalar(hit_one[:, i, :], ramp_h[:, 0:P], slot[1][:, c:c + 1], None, ALU.is_equal)
                           for i, c in enumerate(columns)],
                         *[v.tensor_scalar(to_column[:, q, i, :], ramp_h[:, 0:COLUMNS], column[:, c:c + 1], None,
                                           ALU.is_equal) for i, c in enumerate(columns)])
                    done(*[v.scalar_tensor_tensor(out=to_slot[:, q, i, :], in0=lane_h[:],
                                                  scalar=slot[FLOW_GROUPS][:, c:c + 1], in1=hit_one[:, i, :],
                                                  op0=ALU.is_equal, op1=ALU.add) for i, c in enumerate(columns)])
                    dve.sem_inc(slots_ready, 1)
                dve.wait_ge(used, COLS // AT_ONCE)
                done(v.tensor_scalar(nodes_at[:, 0:COLUMNS], table_ps[:, 0:COLUMNS], float(NODES), None, ALU.add))
                dve.sem_clear(step)

        def emit_find(v, done, keys, found, rounds):
            for r in range(rounds):
                done(v.max(found[:, bass.ts(r, 8)], keys))
                if r + 1 < rounds:
                    done(v.match_replace(keys, found[:, bass.ts(r, 8)], keys, 0.0))

        def emit_stage(v, src, dst, width, k, lows, highs, passing):
            def view(buf, window, ahead_by):
                first, blocks, apart, runs, step_, n = window
                first += ahead_by
                ap = buf[:].unsqueeze(1)
                if blocks > 1:
                    ap = buf[:].rearrange("q (b w) -> q b w", w=apart * width)
                    ap = ap[:, first // apart:first // apart + blocks, :]
                    first %= apart
                if runs > 1:
                    at = first - first % step_
                    ap = ap[:, :, at * width:(at + runs * step_) * width].rearrange("q b (g w) -> q b g w", g=runs)
                    return ap[:, :, :, (first - at) * width:(first - at + n) * width]
                return ap[:, :, first * width:(first + n) * width]

            ops = []
            for slots_, op, to in ((lows, ALU.min, 0), (highs, ALU.max, k)):
                for window in windows(slots_):
                    ops.append(v.tensor_tensor(view(dst, window, to), view(src, window, 0), view(src, window, k), op))
            for part in passing:
                for window in windows(part):
                    ops.append(v.tensor_copy(view(dst, window, 0), view(src, window, 0)))
            return ops

        def emit_sort(v, done, src, dst, width, stages):
            for stage_ in stages:
                done(*emit_stage(v, src, dst, width, *stage_))
                src, dst = dst, src
            return src, dst

        def emit_aggregate(v, done, at, other, weight, agg, first, end, width):
            span = slice(first * width, end * width)
            done(v.tensor_tensor(other[:, span].rearrange("p (k c) -> p k c", c=width),
                                 at[:, span].rearrange("p (k c) -> p k c", c=width),
                                 weight[:, first:end].unsqueeze(2).to_broadcast([P, end - first, width]), ALU.mult))
            done(v.tensor_reduce(agg, other[:, span].rearrange("p (k c) -> p c k", c=width), AX_X, ALU.add))

        def get(eng, semaphore, n=1):
            eng.wait_ge(semaphore, n)
            eng.sem_clear(semaphore)

        cctx = ctx.enter_context(ExitStack())

        def csb(name, shape, dt):
            return cctx.enter_context(nc.sbuf_tensor(name, shape, dt))

        found = csb("found", [P, MAX_FLOW], F32)
        group_row = csb("group_row", [P, 1], F32)
        nbr_next = csb("nbr_next", [P, MAX_FLOW], I32)
        nbr = csb("nbr", [P, MAX_FLOW], I32)
        distance = csb("distance", [P, MAX_FLOW], F32)
        weights = csb("weights", [P, len(TAUS), MAX_FLOW], F32)
        wt_tiles = csb("wt_tiles", [P, len(TAUS)], F32)
        weight = csb("weight", [P, N], F32)
        ids = csb("ids", [P, 1], I32)
        keys_in = csb("keys_in", [P, ROW], F16)
        keys = csb("keys", [P, ROW], F16)
        record = csb("record", [P, META], F32)
        record_next = csb("record_next", [P, META], F32)
        agg = csb("agg", [P, C], F32)
        agg_out = csb("agg_out", [P, C], F32)
        part_row = csb("part_row", [P, 1], F32)
        to_row = csb("to_row", [P, 1], I32)
        out_ids = csb("out_ids", [P, 1], I32)
        gathering = csb("gathering", [P, FLOW_FLOATS], F32)

        HEAD = 2 * C
        assert all(not cap % 2 and cap * C // groups > HEAD for cap, groups in FLOW)

        with ExitStack() as wctx:
            (keys_wanted, keys_landed, keys_free, keys_ready, weights_wanted, weights_ready, go, go_rest, gathered,
             dma_done) = (
                wctx.enter_context(nc.semaphore(n)) for n in (
                    "keys_wanted", "keys_landed", "keys_free", "keys_ready", "weights_wanted", "weights_ready", "go",
                    "go_rest", "gathered", "gather_dmas"))
            act_step, narrow_ready, narrow_joined, rare_stored = (
                wctx.enter_context(nc.semaphore(n)) for n in (
                    "act_step_c", "narrow_ready", "narrow_joined", "rare_stored"))
            join_ps = wctx.enter_context(nc.psum_tensor("join_ps", [P // FLOW_GROUPS, C], F32))
            block = wctx.enter_context(nc.Block())

            @block.sync
            def _(sp):
                sp.dma_start(rare_lists, nodes_at[:, TILES:COLUMNS]).then_inc(
                    rare_stored, 16)
                sp.wait_ge(rare_stored, 16)

            @block.tensor
            def _(pe):
                groups, width = FLOW_GROUPS, C // FLOW_GROUPS
                level = [g for _, g in FLOW].index(groups)
                n = pe.value_load(tiles_of[0:1, level:level + 1], min_val=1, max_val=MOST_TILES)

                def join(_):
                    get(pe, narrow_ready)
                    for g in range(groups):
                        mm = nc.tensor.matmul(join_ps[:, bass.ts(g, width)], ident[:, bass.ts(g, P // groups)],
                                              agg[:, 0:width], start=True, stop=True)
                    mm.then_inc(narrow_joined, 1)
                for_tiles(pe, MOST_TILES, n, join)

            @block.scalar
            def _(act):
                n = act.value_load(tiles_of[0:1, len(LEVELS):len(LEVELS) + 1], min_val=len(FLOW), max_val=MOST_TILES)

                def hand_on(t, is_first=False):
                    get(act, keys_landed)
                    get(act, keys_free)
                    if not is_first:
                        nc.scalar.copy(record_next[:], keys[:, N:ROW].bitcast(F32)).then_inc(act_step, 1)
                        get(act, act_step)
                    nc.scalar.copy(keys[:], keys_in[:]).then_inc(act_step, 1)
                    nc.scalar.copy(ids[:], nodes_at[:, bass.ds(t + 1, 1)]).then_inc(act_step, 1)
                    get(act, act_step, 2)
                    act.sem_inc(keys_ready, 1)
                    act.sem_inc(keys_wanted, 1)
                    if is_first:
                        return
                    get(act, weights_wanted)
                    nc.scalar.copy(record[:], record_next[:]).then_inc(act_step, 1)
                    for i, wt in enumerate(QWEIGHTS):
                        nc.scalar.activation(distance[:], up[:, 0:MAX_FLOW], ACT.Abs,
                                             bias=record_next[:, POSITION + i:POSITION + i + 1]).then_inc(act_step, 1)
                        get(act, act_step, 2 if i == 0 else 1)
                        nc.scalar.activation(weights[:, i, :], distance[:], ACT.Relu, scale=-wt,
                                             bias=wt_tiles[:, i:i + 1]).then_inc(act_step, 1)
                        get(act, act_step)
                    act.sem_inc(weights_ready, 1)

                nc.scalar.copy(ids[:], nodes_at[:, 0:1]).then_inc(act_step, 1)
                get(act, act_step)
                act.sem_inc(keys_wanted, 1)
                hand_on(0, True)
                for_tiles(act, MOST_TILES, n, lambda t: hand_on(t + 1))

            @block.gpsimd
            def _(pool):
                def load_keys():
                    get(pool, keys_wanted)
                    pool.indirect_dma_start(keys_in[:], None, key_rows,
                                            bass.IndirectOffsetOnAxis(ap=ids[:].bitcast(U32), axis=0)).then_inc(
                        dma_done, 16)

                def store_agg():
                    pool.indirect_dma_start(agg_rows, bass.IndirectOffsetOnAxis(ap=out_ids[:].bitcast(U32), axis=0),
                                            agg_out[:], None, bounds_check=NODES - 1, oob_is_err=False).then_inc(
                        dma_done, 16)

                for _ in range(2):
                    load_keys()
                    pool.drain().then_inc(keys_landed, 1)
                for level, (cap, groups) in enumerate(FLOW):
                    width = C // groups
                    rows_of = x1_rows.rearrange("n (g c) -> (n g) c", g=groups)

                    def tile(_, cap=cap, width=width, rows_of=rows_of):
                        get(pool, go)
                        for k in range(cap):
                            if k * width == HEAD:
                                get(pool, go_rest)
                            pool.indirect_dma_start(gathering[:, k * width:(k + 1) * width], None, rows_of,
                                                    bass.IndirectOffsetOnAxis(ap=nbr[:, k:k + 1].bitcast(U32),
                                                                              axis=0)).then_inc(dma_done, 16)
                        store_agg()
                        load_keys()
                        pool.drain().then_inc(gathered, 1)
                        pool.sem_inc(keys_landed, 1)

                    most = NODES * groups // P
                    for_tiles(pool, most, pool.value_load(tiles_of[0:1, level:level + 1], min_val=1, max_val=most),
                              tile)
                for _ in range(2):
                    get(pool, go)
                    store_agg()
                    pool.drain().then_inc(gathered, 1)

            @block.vector
            def _(dve):
                v = nc.vector
                count = [0]

                def done(*instructions):
                    for i in instructions:
                        i.then_inc(step, 1)
                    count[0] += len(instructions)
                    dve.wait_ge(step, count[0])

                def restart():
                    dve.sem_clear(step)
                    count[0] = 0

                def find_neighbours(cap, groups):
                    get(dve, keys_ready)
                    emit_find(v, done, keys[:, 0:N], found, -(-cap // 8))
                    pad_row = keys[:, N:ROW].bitcast(F32)[:, PAD_ROW:PAD_ROW + 1]
                    if groups > 1:
                        done(v.tensor_scalar(group_row[:], pad_row, float(groups), group_f[groups][:, 0:1], ALU.mult,
                                             ALU.add))
                        pad_row = group_row[:, 0:1]
                    done(v.tensor_scalar(nbr_next[:, 0:cap], found[:, 0:cap], float(-groups), pad_row, ALU.mult,
                                         ALU.add))
                    dve.sem_inc(keys_free, 1)

                def hand_over(n):
                    return [v.tensor_copy(nbr[:, 0:n], nbr_next[:, 0:n]), v.tensor_copy(agg_out[:], agg[:]),
                            v.tensor_copy(out_ids[:], to_row[:])]

                def tile(cap, groups, following):
                    width = C // groups
                    if following:
                        find_neighbours(*following)
                    get(dve, gathered)
                    stages, first, end = sort_plan(below(cap), cap)
                    k, lows, highs, _ = stages[0]
                    head, rest = ([[i for i in part if (i * width < HEAD) == is_head] for part in (lows, highs)]
                                  for is_head in (True, False))
                    to_pool = hand_over(following[0] if following else 8)
                    first_part = emit_stage(v, gathering, slots[0], width, k, *head, [])
                    first_part.pop().then_inc(go, 1)
                    done(*to_pool, *first_part, *emit_stage(v, gathering, slots[0], width, k, *rest, []))
                    if following:
                        dve.sem_inc(go_rest, 1)
                    src, dst = emit_sort(v, done, slots[0], slots[1], width, stages[1:])
                    get(dve, weights_ready)
                    done(v.tensor_reduce(weight[:, first:end], weights[:, :, first:end].rearrange("p q k -> p k q"),
                                         AX_X, ALU.add))
                    emit_aggregate(v, done, src, dst, weight, agg[:, 0:width], first, end, width)
                    if groups == 1:
                        done(v.tensor_copy(to_row[:], record[:, NODE:NODE + 1]))
                    else:
                        dve.sem_inc(narrow_ready, 1)
                        done(v.tensor_scalar(part_row[:], record[:, NODE:NODE + 1], float(-NODES), in_lanes[:, 0:1],
                                             ALU.add, ALU.mult))
                        get(dve, narrow_joined)
                        done(v.tensor_copy(agg[0:P // groups, :], join_ps[:]),
                             v.tensor_scalar(to_row[:], part_row[:], float(NODES), None, ALU.add))
                    if following:
                        dve.sem_inc(weights_wanted, 1)
                    restart()

                done(v.memset(to_row[:], NODES), v.memset(agg[:], 0.0), v.memset(nbr_next[:], 0),
                     *[v.memset(wt_tiles[:, i:i + 1], wt) for i, wt in enumerate(QWEIGHTS)])
                dve.sem_inc(keys_free, 1)
                dve.sem_inc(weights_wanted, 1)
                find_neighbours(*FLOW[0])
                done(*hand_over(MAX_FLOW))
                dve.sem_inc(go, 1)
                dve.sem_inc(go_rest, 1)
                restart()
                for level, (cap, groups) in enumerate(FLOW):
                    most = NODES * groups // P
                    n = dve.value_load(tiles_of[0:1, level:level + 1], min_val=1, max_val=most)
                    for_tiles(dve, most - 1, n - 1, lambda _: tile(cap, groups, (cap, groups)), cap <= 24)
                    tile(cap, groups, FLOW[level + 1] if level + 1 < len(FLOW) else None)
                get(dve, gathered)
                done(*hand_over(8))
                dve.sem_inc(go, 1)
                get(dve, gathered)
                restart()

        with ExitStack() as nctx:
            minus = nctx.enter_context(nc.sbuf_tensor("minus", [P, len(TAUS), MAX_FLOW], F32))
            stage = nctx.enter_context(nc.sbuf_tensor("stage", [P, BLOCK, C // min(g for _, g in RARE)], F32))
            ids_free, ids_loaded, tile_loaded, tile_ready, nbr_ready, dma_done, gathered, agg_ready = (
                nctx.enter_context(nc.semaphore(n)) for n in (
                    "ids_free", "ids_loaded", "tile_loaded", "tile_ready", "nbr_ready", "narrow_dmas",
                    "narrow_gathered", "agg_ready"))
            block = nctx.enter_context(nc.Block())

            def each_tile(eng, level, body):
                most = NODES * LEVELS[level][1] // P
                n = eng.value_load(tiles_of[0:1, level:level + 1], min_val=0, max_val=most)
                for_tiles(eng, most, n, body, False)

            @block.sync
            def _(sp):
                for level in range(len(FLOW), len(LEVELS)):
                    groups = LEVELS[level][1]
                    lanes = P // groups
                    per_column = P // lanes
                    start = (level - len(FLOW)) * LIST_COLS

                    def load_ids(i, groups=groups, lanes=lanes, per_column=per_column, start=start):
                        get(sp, ids_free)
                        for g in range(groups):
                            sp.dma_start(ids[bass.ts(g, lanes), :],
                                         rare_lists[bass.ds((i % per_column) * lanes, lanes),
                                                    bass.ds(i // per_column + start, 1)],
                                         allow_slow_non_contiguous=True).then_inc(ids_loaded, 16)
                        get(sp, ids_loaded, 16 * groups)
                        sp.sem_inc(tile_loaded, 1)
                    each_tile(sp, level, load_ids)

            @block.gpsimd
            def _(pool):
                pool.sem_inc(ids_free, 1)
                for level in range(len(FLOW), len(LEVELS)):
                    cap, groups = LEVELS[level]
                    width = C // groups

                    def tile(i, cap=cap, groups=groups, width=width):
                        get(pool, tile_loaded)
                        pool.indirect_dma_start(keys_in[:], None, key_rows,
                                                bass.IndirectOffsetOnAxis(ap=ids[:].bitcast(U32), axis=0)).then_inc(
                            dma_done, 16)
                        pool.drain().then_inc(tile_ready, 1)
                        with pool.Fori(0, cap // BLOCK):
                            get(pool, nbr_ready)
                            for k in range(BLOCK):
                                pool.indirect_dma_start(stage[:].rearrange("p k c -> p (k c)")[:, bass.ts(k, width)],
                                                        None, x1_rows.rearrange("n (g c) -> (n g) c", g=groups),
                                                        bass.IndirectOffsetOnAxis(ap=nbr[:, k:k + 1].bitcast(U32),
                                                                                  axis=0)).then_inc(dma_done, 16)
                            pool.drain().then_inc(gathered, 1)
                        get(pool, agg_ready)
                        pool.indirect_dma_start(agg_rows.rearrange("n (g c) -> (n g) c", g=groups),
                                                bass.IndirectOffsetOnAxis(ap=out_ids[:].bitcast(U32), axis=0),
                                                agg[:, 0:width], None, bounds_check=NODES * groups - 1,
                                                oob_is_err=False).then_inc(dma_done, 16)
                        pool.drain().then_inc(ids_free, 1)
                    each_tile(pool, level, tile)

            @block.vector
            def _(dve):
                v = nc.vector
                count = [0]

                def done(*instructions):
                    for i in instructions:
                        i.then_inc(step, 1)
                    count[0] += len(instructions)
                    dve.wait_ge(step, count[0])

                def restart():
                    dve.sem_clear(step)
                    count[0] = 0

                for level in range(len(FLOW), len(LEVELS)):
                    cap, groups = LEVELS[level]
                    width = C // groups

                    def tile(i, cap=cap, groups=groups, width=width):
                        get(dve, tile_ready)
                        record_in = keys_in[:, N:ROW].bitcast(F32)
                        done(v.tensor_copy(record[:], record_in),
                             v.tensor_scalar(out_ids[:], ids[:], float(groups), group_f[groups][:, 0:1], ALU.mult,
                                             ALU.add))
                        done(v.tensor_scalar(group_row[:], record[:, PAD_ROW:PAD_ROW + 1], float(groups),
                                             group_f[groups][:, 0:1], ALU.mult, ALU.add))
                        restart()
                        with dve.Fori(0, cap // BLOCK) as blk:
                            emit_find(v, done, keys_in[:, 0:N], found, BLOCK // 8)
                            done(v.match_replace(keys_in[:, 0:N], found[:, BLOCK - 8:BLOCK], keys_in[:, 0:N], 0.0),
                                 v.tensor_scalar(nbr[:, 0:BLOCK], found[:, 0:BLOCK], float(-groups),
                                                 group_row[:, 0:1], ALU.mult, ALU.add))
                            dve.sem_inc(nbr_ready, 1)
                            get(dve, gathered)
                            done(v.tensor_copy(slots[0][:, bass.ds(blk * (BLOCK * width), BLOCK * width)],
                                               stage[:].rearrange("p k c -> p (k c)")[:, 0:BLOCK * width]))
                            restart()
                        stages, first, end = sort_plan(below(cap), cap)
                        src, dst = emit_sort(v, done, slots[0], slots[1], width, stages)
                        for at in range(0, cap, MAX_FLOW):
                            done(*[v.tensor_scalar(weights[:, q, :], up[:, at:at + MAX_FLOW],
                                                   record[:, POSITION + q:POSITION + q + 1], None, ALU.add)
                                   for q in range(len(TAUS))])
                            done(v.tensor_scalar(minus[:], weights[:], -1.0, None, ALU.mult))
                            done(v.tensor_tensor(weights[:], weights[:], minus[:], ALU.max))
                            done(*[v.tensor_scalar(weights[:, q, :], weights[:, q, :], -wt, wt, ALU.mult, ALU.add)
                                   for q, wt in enumerate(QWEIGHTS)])
                            done(v.tensor_scalar(weights[:], weights[:], 0.0, None, ALU.max))
                            done(v.tensor_reduce(weight[:, at:at + MAX_FLOW],
                                                 weights[:].rearrange("p q k -> p k q"), AX_X, ALU.add))
                        emit_aggregate(v, done, src, dst, weight, agg[:, 0:width], first, end, width)
                        dve.sem_inc(agg_ready, 1)
                        restart()
                    each_tile(dve, level, tile)

        with ExitStack() as dctx:
            def dsb(name, shape, dt):
                return dctx.enter_context(nc.sbuf_tensor(name, shape, dt))

            def dsem(name):
                return dctx.enter_context(nc.semaphore(name))

            x1_in, agg_in = (slots[i][:, 0:B * T * C].rearrange("p (b t c) -> p b t c", b=B, t=T) for i in range(2))
            res = [dsb(f"res{i}", [P, T, C], F32) for i in range(2)]
            resT = dsb("resT", [C, N], F32)
            hidT = dsb("hidT", [H, N], F32)
            y = dsb("y", [P, T, C], F32)
            cen = dsb("cen", [P, T, C], F32)
            sq = dsb("sq", [P, T, C], F32)
            mean = dsb("mean_d", [P, T], F32)
            var = dsb("var_d", [P, T], F32)
            rstd = dsb("rstd_d", [P, T], F32)
            fin = [dsb(f"fin{i}", [P, T, C], F32) for i in range(2)]
            resT_ps = dctx.enter_context(nc.psum_tensor("resT_ps", [C, N], F32))
            hid_ps = dctx.enter_context(nc.psum_tensor("hid_ps", [H, N], F32))
            out_ps = dctx.enter_context(nc.psum_tensor("out_ps", [P, T, C], F32))
            in_loaded = [dsem(f"in_loaded{b}") for b in range(B)]
            fin_stored = [dsem(f"fin_stored{i}") for i in range(2)]
            (res_ready, resT_ready, resT_copied, hid_ready, hid_act, out_ready, y_done, var_ready, rstd_ready,
             fin_ready) = (dsem(n) for n in (
                 "res_ready", "resT_ready", "resT_copied", "hid_ready", "hid_act", "out_ready", "y_done",
                 "var_ready_d", "rstd_ready_d", "fin_ready"))
            block = dctx.enter_context(nc.Block())

            @block.sync
            def _(sp):
                for b in range(B):
                    for dst, src, first in ((x1_in, x1_rows, b * (N + 1)), (agg_in, agg_rows, b * N)):
                        sp.dma_start(dst[:, b], rows(src, first, N).rearrange("(t p) c -> p t c", p=P)).then_inc(
                            in_loaded[b], 16)
                for b in range(B):
                    sp.wait_ge(fin_ready, b + 1)
                    sp.dma_start(out[b].rearrange("(t p) c -> p t c", p=P), fin[b % 2][:]).then_inc(
                        fin_stored[b % 2], 16)
                for q in range(2):
                    sp.wait_ge(fin_stored[q], 16 * (B // 2))

            @block.tensor
            def _(pe):
                def turn_res(b):
                    pe.wait_ge(res_ready, b + 1)
                    for t in range(T):
                        mm = nc.tensor.transpose(resT_ps[:, bass.ts(t, P)], res[b % 2][:, t, :], ident[:])
                    mm.then_inc(resT_ready, 1)

                turn_res(0)
                for b in range(B):
                    pe.wait_ge(resT_copied, b + 1)
                    for h in range(2):
                        mm = nc.tensor.matmul(hid_ps[:, bass.ts(h, 512)], W1_sb[:], resT[:, bass.ts(h, 512)],
                                              start=True, stop=True)
                    mm.then_inc(hid_ready, 1)
                    if b + 1 < B:
                        turn_res(b + 1)
                    pe.wait_ge(hid_act, b + 1)
                    if b:
                        pe.wait_ge(y_done, b)
                    for t in range(T):
                        mm = nc.tensor.matmul(out_ps[:, t, :], hidT[:, bass.ts(t, P)], W2_sb[:], start=True, stop=True)
                    mm.then_inc(out_ready, 1)

            @block.scalar
            def _(act):
                def copy_res(b):
                    act.wait_ge(resT_ready, b + 1)
                    nc.scalar.copy(resT[:], resT_ps[:]).then_inc(resT_copied, 1)

                copy_res(0)
                for b in range(B):
                    act.wait_ge(hid_ready, b + 1)
                    nc.scalar.activation(hidT[:], hid_ps[:], ACT.Relu, bias=b1_sb[:, 0:1]).then_inc(hid_act, 1)
                    if b + 1 < B:
                        copy_res(b + 1)

            @block.gpsimd
            def _(pool):
                for b in range(B):
                    pool.wait_ge(var_ready, b + 1)
                    nc.gpsimd.tensor_tensor(rstd[:], var[:], power[:], ALU.pow).then_inc(rstd_ready, 1)

            @block.vector
            def _(dve):
                v = nc.vector
                count = [0]

                def done(*instructions):
                    for i in instructions:
                        i.then_inc(step, 1)
                    count[0] += len(instructions)
                    dve.wait_ge(step, count[0])

                def wide(ap):
                    return ap.unsqueeze(2).to_broadcast([P, T, C])

                def make_res(b):
                    dve.wait_ge(in_loaded[b], 32)
                    if b >= 2:
                        dve.wait_ge(out_ready, b - 1)
                    done(v.tensor_tensor(res[b % 2][:], x1_in[:, b], agg_in[:, b], ALU.add))
                    dve.sem_inc(res_ready, 1)

                def finish(b):
                    dve.wait_ge(rstd_ready, b + 1)
                    if b >= 2:
                        dve.wait_ge(fin_stored[b % 2], 16 * (b // 2))
                    done(v.tensor_tensor(fin[b % 2][:], cen[:], wide(rstd[:]), ALU.mult))
                    dve.sem_inc(fin_ready, 1)

                make_res(0)
                make_res(1)
                for b in range(B):
                    dve.wait_ge(out_ready, b + 1)
                    done(v.tensor_tensor(y[:], out_ps[:], b2_sb[:].unsqueeze(1).to_broadcast([P, T, C]), ALU.add))
                    dve.sem_inc(y_done, 1)
                    if b + 2 < B:
                        make_res(b + 2)
                    if b:
                        finish(b - 1)
                    done(v.tensor_tensor(y[:], y[:], wide(mask_f[:, b * T:(b + 1) * T]), ALU.mult))
                    done(v.tensor_tensor(y[:], y[:], x1_in[:, b], ALU.add))
                    done(v.tensor_reduce(mean[:], y[:], AX_X, ALU.add))
                    done(v.tensor_scalar(mean[:], mean[:], 1.0 / C, None, ALU.mult))
                    done(v.tensor_tensor(cen[:], y[:], wide(mean[:]), ALU.subtract))
                    done(v.tensor_tensor(sq[:], cen[:], cen[:], ALU.mult))
                    done(v.tensor_reduce(var[:], sq[:], AX_X, ALU.add))
                    done(v.tensor_scalar(var[:], var[:], 1.0 / C, EPS, ALU.mult, ALU.add))
                    dve.sem_inc(var_ready, 1)
                finish(B - 1)


def kernel(x, adj, nodemask, L0_gnn_weight, L0_gnn_bias, L1_gnn_W1, L1_gnn_b1, L1_gnn_W2, L1_gnn_b2):
    import numpy as np
    import concourse.bacc as bacc
    from concourse.bass_utils import run_bass_kernel_spmd

    x = np.asarray(x)
    adj = np.asarray(adj)
    mask = np.asarray(nodemask).view(np.uint8)
    w0 = np.asarray(L0_gnn_weight)
    C = x.shape[2]
    data = {
        "x": x,
        "xT": x.transpose(0, 2, 1),
        "adj": adj,
        "mask": mask.reshape(-1, P).T,
        "w_cat": w0[:, 0].transpose(1, 0, 2).reshape(C, -1),
        "bias0": np.asarray(L0_gnn_bias).reshape(-1),
        "W1": np.asarray(L1_gnn_W1),
        "b1": np.asarray(L1_gnn_b1).reshape(-1, 1),
        "W2": np.asarray(L1_gnn_W2),
        "b2": np.asarray(L1_gnn_b2).reshape(-1),
    }
    data = {f"in_{k}": np.ascontiguousarray(a) for k, a in data.items()}
    nc = bacc.Bacc("TRN2", target_bir_lowering=False, num_devices=1)
    args = [nc.dram_tensor(k, a.shape, mybir.dt.from_np(a.dtype), kind="ExternalInput").ap() for k, a in data.items()]
    out = nc.dram_tensor("out", x.shape, F32, kind="ExternalOutput").ap()
    build(nc, *args, out)
    result = run_bass_kernel_spmd(nc, [data], core_ids=[0])
    return result.results[0]["out"]
```
